# Optimizing a Trainium2 kernel written in Bass

```python
import numpy as np
import jax
import jax.numpy as jnp

def _softmax(x, axis=-1):
    return jax.nn.softmax(x, axis=axis)

def _gelu(x):
    return jax.nn.gelu(x, approximate=True)

def _silu(x):
    return jax.nn.silu(x)

def _sigmoid(x):
    return jax.nn.sigmoid(x)

def _layernorm(x, axis=-1, eps=1e-05):
    m = jnp.mean(x, axis=axis, keepdims=True)
    v = jnp.var(x, axis=axis, keepdims=True)
    return (x - m) / jnp.sqrt(v + eps)

def _scatter_add(tgt, idx, src, axis=0):
    return tgt.at[idx].add(src)

def _segment_sum(src, seg, n):
    return jax.ops.segment_sum(src, seg, n)
kernel_name = 'mk_adaln_d1_jaxref_r2_ef78fc'

def setup_inputs(seed: int=0):
    np.random.seed(seed)
    _w = jnp.asarray

    def _L0_attn_setup():
        import jax, jax.numpy as jnp
        import numpy as np
        B_, L_, DM = (2, 1024, 512)
        DS, DC, EXP, HD = (128, 4, 2, 64)
        DI = EXP * DM
        NH = DI // HD
        CONV_DIM = DI + 2 * DS
        DIN = 2 * DI + 2 * DS + NH
        CS = 128
        EPS = 1e-05

        def _segsum(a):
            T = a.shape[-1]
            cs = jnp.cumsum(a, -1)
            seg = cs[..., :, None] - cs[..., None, :]
            mask = jnp.tril(jnp.ones((T, T), bool))
            return jnp.where(mask, seg, -jnp.inf)

        def _ssd(X, A, Bm, Cm):
            b, l, h, p = X.shape
            n, nc = (Bm.shape[-1], l // CS)
            X = X.reshape(b, nc, CS, h, p)
            A = A.reshape(b, nc, CS, h).transpose(0, 3, 1, 2)
            Bm = Bm.reshape(b, nc, CS, n)
            Cm = Cm.reshape(b, nc, CS, n)
            Acs = jnp.cumsum(A, -1)
            Lmat = jnp.exp(_segsum(A))
            Y_diag = jnp.einsum('bcln,bcsn,bhcls,bcshp->bclhp', Cm, Bm, Lmat, X)
            decay_states = jnp.exp(Acs[..., -1:] - Acs)
            states = jnp.einsum('bcln,bhcl,bclhp->bchpn', Bm, decay_states, X)
            states = jnp.concatenate([jnp.zeros_like(states[:, :1]), states], axis=1)
            decay_chunk = jnp.exp(_segsum(jnp.pad(Acs[..., -1], ((0, 0), (0, 0), (1, 0)))))
            states = jnp.einsum('bhzc,bchpn->bzhpn', decay_chunk, states)[:, :-1]
            Y_off = jnp.einsum('bcln,bchpn,bhcl->bclhp', Cm, states, jnp.exp(Acs))
            return (Y_diag + Y_off).reshape(b, l, h, p)

        def _forward(x, norm_w, in_proj_w, conv_w, conv_b, dt_bias, A_log, D, gnorm_w, out_proj_w):
            b, l, _ = x.shape
            xn = x * jax.lax.rsqrt(jnp.mean(x * x, -1, keepdims=True) + EPS) * norm_w
            zxbcdt = jnp.einsum('bld,ed->ble', xn, in_proj_w)
            z = zxbcdt[..., :DI]
            xBC = zxbcdt[..., DI:DI + CONV_DIM]
            dt = zxbcdt[..., -NH:]
            pad = jnp.pad(xBC, ((0, 0), (DC - 1, 0), (0, 0)))
            conv = sum((pad[:, k:k + l, :] * conv_w[:, k] for k in range(DC))) + conv_b
            xBC = conv * jax.nn.sigmoid(conv)
            xs = xBC[..., :DI]
            Bm = xBC[..., DI:DI + DS]
            Cm = xBC[..., DI + DS:]
            dt = jax.nn.softplus(dt + dt_bias)
            A = -jnp.exp(A_log)
            xh = xs.reshape(b, l, NH, HD)
            y = _ssd(xh * dt[..., None], dt * A, Bm, Cm)
            y = y + D[None, None, :, None] * xh
            y = y.reshape(b, l, DI)
            y = y * (z * jax.nn.sigmoid(z))
            y = y * jax.lax.rsqrt(jnp.mean(y * y, -1, keepdims=True) + EPS) * gnorm_w
            return x + jnp.einsum('bld,ed->ble', y, out_proj_w)
        key = jax.random.key(seed)
        ks = jax.random.split(key, 8)
        s = 0.02
        x = jax.random.normal(ks[0], (B_, L_, DM), jnp.float32)
        norm_w = jnp.ones((DM,), jnp.float32)
        in_proj_w = jax.random.normal(ks[1], (DIN, DM), jnp.float32) * s
        conv_w = jax.random.normal(ks[2], (CONV_DIM, DC), jnp.float32) * 0.2
        conv_b = jnp.zeros((CONV_DIM,), jnp.float32)
        dt_bias = jnp.log(jnp.expm1(jax.random.uniform(ks[3], (NH,), minval=0.001, maxval=0.1)))
        A_log = jnp.log(jax.random.uniform(ks[4], (NH,), minval=1.0, maxval=16.0))
        D = jnp.ones((NH,), jnp.float32)
        gnorm_w = jnp.ones((DI,), jnp.float32)
        out_proj_w = jax.random.normal(ks[5], (DM, DI), jnp.float32) * s
        return dict(x=x, norm_w=norm_w, in_proj_w=in_proj_w, conv_w=conv_w, conv_b=conv_b, dt_bias=dt_bias, A_log=A_log, D=D, gnorm_w=gnorm_w, out_proj_w=out_proj_w)
    _L0_attn_in = _L0_attn_setup()

    def _L0_ffn_setup():
        import jax, jax.numpy as jnp
        import numpy as np
        N_GROUP = 8
        TOPK_GROUP = 4
        TOPK = 8
        ROUTED_SCALE = 2.5
        B, S, D, F, E = (4, 1024, 512, 256, 64)

        def _route(x, w_router, b_router):
            scores = jax.nn.sigmoid(jnp.einsum('bsd,de->bse', x, w_router)).astype(jnp.float32)
            swb = scores + b_router
            e = scores.shape[-1]
            group_scores = jnp.sum(jax.lax.top_k(swb.reshape(swb.shape[:-1] + (N_GROUP, -1)), 2)[0], axis=-1)
            group_idx = jax.lax.top_k(group_scores, TOPK_GROUP)[1]
            mask = jnp.any(jnp.arange(N_GROUP)[:, None] == group_idx[..., None, :], axis=-1)
            mask = jnp.repeat(mask, e // N_GROUP, axis=-1)
            masked_scores = jnp.where(mask, swb, 0.0)
            topk_idx = jax.lax.top_k(masked_scores, TOPK)[1]
            topk_w = jnp.take_along_axis(scores, topk_idx, axis=-1).astype(jnp.float32)
            topk_w = ROUTED_SCALE * topk_w / (jnp.sum(topk_w, axis=-1)[..., None] + 1e-20)
            return (topk_w, topk_idx)

        def _moe_forward(x, w_router, b_router, we_gate, we_up, we_down, ws_gate, ws_up, ws_down):
            b, s, d = x.shape
            e = we_gate.shape[0]
            topk_w, topk_idx = _route(x, w_router, b_router)
            x_flat = x.reshape(-1, d)
            idx_flat = topk_idx.reshape(-1)
            sort = jnp.argsort(idx_flat)
            tok = sort // TOPK
            x_sorted = x_flat[tok]
            group_sizes = jnp.bincount(idx_flat, length=e).astype(jnp.int32)
            g = jax.lax.ragged_dot(x_sorted, we_gate, group_sizes)
            u = jax.lax.ragged_dot(x_sorted, we_up, group_sizes)
            o = jax.lax.ragged_dot(jax.nn.silu(g) * u, we_down, group_sizes)
            w_sorted = topk_w.reshape(-1)[sort].astype(o.dtype)
            y = jnp.zeros_like(x_flat).at[tok].add(o * w_sorted[:, None])
            y = y.reshape(b, s, d)
            shared = jnp.einsum('btf,fd->btd', jax.nn.silu(jnp.einsum('btd,df->btf', x, ws_gate)) * jnp.einsum('btd,df->btf', x, ws_up), ws_down)
            return y + shared
        key = jax.random.key(seed)
        ks = jax.random.split(key, 10)
        sd = 1.0 / np.sqrt(D)
        sf = 1.0 / np.sqrt(F)
        return {'x': jax.random.normal(ks[0], (B, S, D), jnp.float32), 'w_router': jax.random.normal(ks[1], (D, E), jnp.float32) * sd, 'b_router': jax.random.normal(ks[2], (E,), jnp.float32) * 0.1, 'we_gate': jax.random.normal(ks[3], (E, D, F), jnp.float32) * sd, 'we_up': jax.random.normal(ks[4], (E, D, F), jnp.float32) * sd, 'we_down': jax.random.normal(ks[5], (E, F, D), jnp.float32) * sf, 'ws_gate': jax.random.normal(ks[6], (D, F), jnp.float32) * sd, 'ws_up': jax.random.normal(ks[7], (D, F), jnp.float32) * sd, 'ws_down': jax.random.normal(ks[8], (F, D), jnp.float32) * sf}
    _L0_ffn_in = _L0_ffn_setup()
    _L0_c = _w((lambda *s: np.random.randn(*s).astype(np.float32) * 0.05)(4, 512))
    _L0_wmod = _w((lambda *s: np.random.randn(*s).astype(np.float32) * 0.05)(512, 6 * 512) * 512 ** (-0.5))
    _d = {'L0_attn_x': _L0_attn_in['x'], 'L0_attn_norm_w': _L0_attn_in['norm_w'], 'L0_attn_in_proj_w': _L0_attn_in['in_proj_w'], 'L0_attn_conv_w': _L0_attn_in['conv_w'], 'L0_attn_conv_b': _L0_attn_in['conv_b'], 'L0_attn_dt_bias': _L0_attn_in['dt_bias'], 'L0_attn_A_log': _L0_attn_in['A_log'], 'L0_attn_D': _L0_attn_in['D'], 'L0_attn_gnorm_w': _L0_attn_in['gnorm_w'], 'L0_attn_out_proj_w': _L0_attn_in['out_proj_w'], 'L0_ffn_w_router': _L0_ffn_in['w_router'], 'L0_ffn_b_router': _L0_ffn_in['b_router'], 'L0_ffn_we_gate': _L0_ffn_in['we_gate'], 'L0_ffn_we_up': _L0_ffn_in['we_up'], 'L0_ffn_we_down': _L0_ffn_in['we_down'], 'L0_ffn_ws_gate': _L0_ffn_in['ws_gate'], 'L0_ffn_ws_up': _L0_ffn_in['ws_up'], 'L0_ffn_ws_down': _L0_ffn_in['ws_down'], 'L0_c': _L0_c, 'L0_wmod': _L0_wmod}
    _x0 = _d['L0_attn_x']
    _d['L0_attn_x'] = jax.random.normal(jax.random.fold_in(jax.random.key(seed), 1), (4, 2048, 512), dtype=_x0.dtype)
    del _x0
    return _d

def reference(L0_attn_x, L0_attn_norm_w, L0_attn_in_proj_w, L0_attn_conv_w, L0_attn_conv_b, L0_attn_dt_bias, L0_attn_A_log, L0_attn_D, L0_attn_gnorm_w, L0_attn_out_proj_w, L0_ffn_w_router, L0_ffn_b_router, L0_ffn_we_gate, L0_ffn_we_up, L0_ffn_we_down, L0_ffn_ws_gate, L0_ffn_ws_up, L0_ffn_ws_down, L0_c, L0_wmod):

    def _L0_attn_ref(x, norm_w, in_proj_w, conv_w, conv_b, dt_bias, A_log, D, gnorm_w, out_proj_w):
        import jax, jax.numpy as jnp
        import numpy as np
        B_, L_, DM = (2, 1024, 512)
        DS, DC, EXP, HD = (128, 4, 2, 64)
        DI = EXP * DM
        NH = DI // HD
        CONV_DIM = DI + 2 * DS
        DIN = 2 * DI + 2 * DS + NH
        CS = 128
        EPS = 1e-05

        def _segsum(a):
            T = a.shape[-1]
            cs = jnp.cumsum(a, -1)
            seg = cs[..., :, None] - cs[..., None, :]
            mask = jnp.tril(jnp.ones((T, T), bool))
            return jnp.where(mask, seg, -jnp.inf)

        def _ssd(X, A, Bm, Cm):
            b, l, h, p = X.shape
            n, nc = (Bm.shape[-1], l // CS)
            X = X.reshape(b, nc, CS, h, p)
            A = A.reshape(b, nc, CS, h).transpose(0, 3, 1, 2)
            Bm = Bm.reshape(b, nc, CS, n)
            Cm = Cm.reshape(b, nc, CS, n)
            Acs = jnp.cumsum(A, -1)
            Lmat = jnp.exp(_segsum(A))
            Y_diag = jnp.einsum('bcln,bcsn,bhcls,bcshp->bclhp', Cm, Bm, Lmat, X)
            decay_states = jnp.exp(Acs[..., -1:] - Acs)
            states = jnp.einsum('bcln,bhcl,bclhp->bchpn', Bm, decay_states, X)
            states = jnp.concatenate([jnp.zeros_like(states[:, :1]), states], axis=1)
            decay_chunk = jnp.exp(_segsum(jnp.pad(Acs[..., -1], ((0, 0), (0, 0), (1, 0)))))
            states = jnp.einsum('bhzc,bchpn->bzhpn', decay_chunk, states)[:, :-1]
            Y_off = jnp.einsum('bcln,bchpn,bhcl->bclhp', Cm, states, jnp.exp(Acs))
            return (Y_diag + Y_off).reshape(b, l, h, p)

        def _forward(x, norm_w, in_proj_w, conv_w, conv_b, dt_bias, A_log, D, gnorm_w, out_proj_w):
            b, l, _ = x.shape
            xn = x * jax.lax.rsqrt(jnp.mean(x * x, -1, keepdims=True) + EPS) * norm_w
            zxbcdt = jnp.einsum('bld,ed->ble', xn, in_proj_w)
            z = zxbcdt[..., :DI]
            xBC = zxbcdt[..., DI:DI + CONV_DIM]
            dt = zxbcdt[..., -NH:]
            pad = jnp.pad(xBC, ((0, 0), (DC - 1, 0), (0, 0)))
            conv = sum((pad[:, k:k + l, :] * conv_w[:, k] for k in range(DC))) + conv_b
            xBC = conv * jax.nn.sigmoid(conv)
            xs = xBC[..., :DI]
            Bm = xBC[..., DI:DI + DS]
            Cm = xBC[..., DI + DS:]
            dt = jax.nn.softplus(dt + dt_bias)
            A = -jnp.exp(A_log)
            xh = xs.reshape(b, l, NH, HD)
            y = _ssd(xh * dt[..., None], dt * A, Bm, Cm)
            y = y + D[None, None, :, None] * xh
            y = y.reshape(b, l, DI)
            y = y * (z * jax.nn.sigmoid(z))
            y = y * jax.lax.rsqrt(jnp.mean(y * y, -1, keepdims=True) + EPS) * gnorm_w
            return x + jnp.einsum('bld,ed->ble', y, out_proj_w)
        return _forward(x, norm_w, in_proj_w, conv_w, conv_b, dt_bias, A_log, D, gnorm_w, out_proj_w)

    def _L0_ffn_ref(x, w_router, b_router, we_gate, we_up, we_down, ws_gate, ws_up, ws_down):
        import jax, jax.numpy as jnp
        import numpy as np
        N_GROUP = 8
        TOPK_GROUP = 4
        TOPK = 8
        ROUTED_SCALE = 2.5
        B, S, D, F, E = (4, 1024, 512, 256, 64)

        def _route(x, w_router, b_router):
            scores = jax.nn.sigmoid(jnp.einsum('bsd,de->bse', x, w_router)).astype(jnp.float32)
            swb = scores + b_router
            e = scores.shape[-1]
            group_scores = jnp.sum(jax.lax.top_k(swb.reshape(swb.shape[:-1] + (N_GROUP, -1)), 2)[0], axis=-1)
            group_idx = jax.lax.top_k(group_scores, TOPK_GROUP)[1]
            mask = jnp.any(jnp.arange(N_GROUP)[:, None] == group_idx[..., None, :], axis=-1)
            mask = jnp.repeat(mask, e // N_GROUP, axis=-1)
            masked_scores = jnp.where(mask, swb, 0.0)
            topk_idx = jax.lax.top_k(masked_scores, TOPK)[1]
            topk_w = jnp.take_along_axis(scores, topk_idx, axis=-1).astype(jnp.float32)
            topk_w = ROUTED_SCALE * topk_w / (jnp.sum(topk_w, axis=-1)[..., None] + 1e-20)
            return (topk_w, topk_idx)

        def _moe_forward(x, w_router, b_router, we_gate, we_up, we_down, ws_gate, ws_up, ws_down):
            b, s, d = x.shape
            e = we_gate.shape[0]
            topk_w, topk_idx = _route(x, w_router, b_router)
            x_flat = x.reshape(-1, d)
            idx_flat = topk_idx.reshape(-1)
            sort = jnp.argsort(idx_flat)
            tok = sort // TOPK
            x_sorted = x_flat[tok]
            group_sizes = jnp.bincount(idx_flat, length=e).astype(jnp.int32)
            g = jax.lax.ragged_dot(x_sorted, we_gate, group_sizes)
            u = jax.lax.ragged_dot(x_sorted, we_up, group_sizes)
            o = jax.lax.ragged_dot(jax.nn.silu(g) * u, we_down, group_sizes)
            w_sorted = topk_w.reshape(-1)[sort].astype(o.dtype)
            y = jnp.zeros_like(x_flat).at[tok].add(o * w_sorted[:, None])
            y = y.reshape(b, s, d)
            shared = jnp.einsum('btf,fd->btd', jax.nn.silu(jnp.einsum('btd,df->btf', x, ws_gate)) * jnp.einsum('btd,df->btf', x, ws_up), ws_down)
            return y + shared
        return _moe_forward(x, w_router, b_router, we_gate, we_up, we_down, ws_gate, ws_up, ws_down)
    x = L0_attn_x
    mod = (_silu(L0_c) @ L0_wmod).reshape(L0_c.shape[0], 6, 1, -1)
    sa, ca, ga, sb, cb, gb = (mod[:, 0], mod[:, 1], mod[:, 2], mod[:, 3], mod[:, 4], mod[:, 5])
    ga = (2 * (ga >= 0) - 1) * jnp.maximum(jnp.abs(ga), 0.25)
    gb = (2 * (gb >= 0) - 1) * jnp.maximum(jnp.abs(gb), 0.25)
    h = _layernorm(x, axis=-1) * (1 + ca) + sa
    x = x + ga * _L0_attn_ref(h, L0_attn_norm_w, L0_attn_in_proj_w, L0_attn_conv_w, L0_attn_conv_b, L0_attn_dt_bias, L0_attn_A_log, L0_attn_D, L0_attn_gnorm_w, L0_attn_out_proj_w)
    h = _layernorm(x, axis=-1) * (1 + cb) + sb
    x = x + gb * _L0_ffn_ref(h, L0_ffn_w_router, L0_ffn_b_router, L0_ffn_we_gate, L0_ffn_we_up, L0_ffn_we_down, L0_ffn_ws_gate, L0_ffn_ws_up, L0_ffn_ws_down)
    return x

_drawn_inputs = setup_inputs


def setup_inputs(seed=0):
    import zlib

    import numpy as np

    out = dict(_drawn_inputs(seed))
    spreads = {'L0_attn_norm_w': (1.0, 0.2),
     'L0_attn_conv_b': (0.0, 0.1),
     'L0_attn_D': (1.0, 0.2),
     'L0_attn_gnorm_w': (1.0, 0.2)}
    factors = {}
    for name, (base, spread) in spreads.items():
        noise = np.random.default_rng([zlib.crc32(name.encode()), seed]).standard_normal(out[name].shape)
        drawn = base * np.exp(spread * noise) if base else spread * noise
        out[name] = jnp.asarray(drawn.astype(out[name].dtype))
    for name, factor in factors.items():
        out[name] = (out[name] * factor).astype(out[name].dtype)
    return out
```

```python
import concourse.bass as bass
from concourse import mybir
from contextlib import ExitStack

FP32 = mybir.dt.float32
I32 = mybir.dt.int32
U32 = mybir.dt.uint32
ALU = mybir.AluOpType
ACT = mybir.ActivationFunctionType
AX = mybir.AxisListType

P = 128
BATCH, SEQ, DM = 4, 2048, 512
TOKENS = BATCH * SEQ
NCH = TOKENS // P
CPB = SEQ // P
KD = DM // P
DI = 1024
KI = DI // P
NH, HD = 16, 64
NE = 10
TAPS = 4
DIN = 2 * DI + 2 * P + NH
EXPERTS, TOPK, FF = 64, 8, 256
GROUPS, TOPG = 8, 4
KF = FF // P
WPE = KD * 2 * FF + KF * DM
LN_EPS = 1e-5
ROUTED_SCALE = 2.5
NBLK = TOKENS * TOPK // P + EXPERTS
SEG = TOKENS
LIST = EXPERTS * SEG + EXPERTS * P
LCOLS = LIST // P


def wait_apart(eng, sem, value, passed):
    eng.wait_ge(sem, value)
    eng.sem_inc(passed, 1)


def at_least(eng, sem, value):
    if isinstance(value, int) and value <= 0:
        return
    eng.wait_ge(sem, value)


class Order:

    def __init__(self, eng, sem, per):
        self.eng, self.sem, self.per = eng, sem, per

    def begin(self, chunk):
        self.base, self.n = chunk * self.per, 0

    def mark(self, ins):
        ins.then_inc(self.sem, 1)
        self.n += 1
        return self.n

    def wait(self, n=None):
        self.eng.wait_ge(self.sem, self.base + (self.n if n is None else n))

    def wait_apart(self, passed):
        wait_apart(self.eng, self.sem, self.base + self.n, passed)

    def end(self):
        assert self.n == self.per, (self.n, self.per)


def program(nc, x, c_t, w_mod, w_in, conv_w, conv_b, dt_bias, a_log, d_skip, norm_w, gnorm_w,
            w_out, w_router, b_router, w_experts, w_shared, out):
    mod_dram = nc.dram_tensor("mod_dram", (BATCH, 6 * DM), FP32, kind="Internal").ap()
    x1_dram = nc.dram_tensor("x1_dram", (TOKENS, DM), FP32, kind="Internal").ap()
    h2_dram = nc.dram_tensor("h2_dram", (TOKENS, DM), FP32, kind="Internal").ap()
    list_dram = nc.dram_tensor("list_dram", (LIST, 1), FP32, kind="Internal").ap()
    y_dram = nc.dram_tensor("y_dram", (NBLK * P, DM), FP32, kind="Internal").ap()

    with ExitStack() as top:
        sems = {}

        def sem(name):
            sems[name] = top.enter_context(nc.semaphore(name))
            return sems[name]

        def tile(stack, name, shape, dt=FP32):
            return stack.enter_context(nc.sbuf_tensor(name, shape, dt))

        bank = [top.enter_context(nc.psum_tensor(f"bank{i}", [P, 1024], FP32)) for i in range(4)]

        def half(i):
            return bank[i // 2][:, (i % 2) * 512:(i % 2) * 512 + 512]

        ident = tile(top, "ident", [P, P])
        tri = tile(top, "tri", [P, P])
        tri_strict = tile(top, "tri_strict", [P, P])
        ones = tile(top, "ones", [P, P])
        iota_e = tile(top, "iota_e", [P, EXPERTS])
        iota_p = tile(top, "iota_p", [P, 1])
        
        top_e = tile(top, "top_e", [P, NCH, TOPK])
        top_r = tile(top, "top_r", [P, NCH, TOPK])
        top_w = tile(top, "top_w", [P, NCH, TOPK])
        count = tile(top, "count", [P, EXPERTS])

        mixer(nc, top, sem, tile, bank, half, locals())
        route_tables = tables(nc, top, sem, tile, bank, half, locals())
        experts(nc, top, sem, tile, bank, half, locals(), route_tables)
        combine(nc, top, sem, tile, bank, half, locals(), route_tables)


def mixer(nc, top, sem, tile, bank, half, env):
    (x, c_t, w_mod_d, w_in_d, conv_w_d, conv_b_d, dt_bias_d, a_log_d, d_skip_d, norm_w_d,
     gnorm_w_d, w_out_d, w_router_d, b_router_d) = (env[k] for k in (
         "x", "c_t", "w_mod", "w_in", "conv_w", "conv_b", "dt_bias", "a_log", "d_skip", "norm_w",
         "gnorm_w", "w_out", "w_router", "b_router"))
    mod_dram, x1_dram, h2_dram, list_dram = (env[k] for k in ("mod_dram", "x1_dram", "h2_dram", "list_dram"))
    ident, tri, tri_strict, ones, iota_e, iota_p, top_e, top_r, top_w, count = (env[k] for k in (
        "ident", "tri", "tri_strict", "ones", "iota_e", "iota_p", "top_e", "top_r", "top_w", "count"))

    with ExitStack() as ph:
        def sb(name, shape, dt=FP32):
            return tile(ph, name, shape, dt)

        mod = sb("mod", [P, BATCH, 5, DM])
        w_in = sb("w_in", [P, KD, DIN])
        w_out = sb("w_out", [P, KI, DM])
        conv_w = sb("conv_w", [P, NE, TAPS])
        conv_b = sb("conv_b", [P, NE])
        dt_bias = sb("dt_bias", [P, NH])
        a_neg = sb("a_neg", [P, NH])
        d_skip = sb("d_skip", [P, NH])
        norm_w = sb("norm_w", [P, KD])
        gnorm_w = sb("gnorm_w", [P, KI])
        w_router = sb("w_router", [P, KD, EXPERTS])
        b_router = sb("b_router", [P, EXPERTS])
        starts = sb("starts", [P, NCH])
        ends = sb("ends", [P, NCH])
        raw = sb("raw", [P, 2, NE, TAPS - 1 + P])
        state = sb("state", [P, DI])
        tok_id = sb("tok_id", [P, 2])
        minus_half = sb("minus_half", [P, 1])

        s_load = sem("s_load")
        s_const = sem("s_const")
        s_iota = sem("s_iota")
        
        s_mod = sem("s_mod")
        s_setup = sem("s_setup")
        s_act_set = sem("s_act_set")
        s_pe_set = sem("s_pe_set")

        with ExitStack() as st:
            c_in = tile(st, "c_in", [P, KD, BATCH])
            c_tanh = tile(st, "c_tanh", [P, KD, BATCH])
            c_silu = tile(st, "c_silu", [P, KD, BATCH])
            w_mod = tile(st, "w_mod_sb", [P, KD, 3, DM])
            mod_row = tile(st, "mod_row", [BATCH, 6, DM])
            mod_abs = tile(st, "mod_abs", [BATCH, DM])
            mod_sign = tile(st, "mod_sign", [BATCH, DM])
            zeros = tile(st, "zeros", [P, LCOLS])
            w_mod_dh = w_mod_d.rearrange("p k (a n) -> p k a n", a=2)
            s_wmod = [sem("s_wmod0"), sem("s_wmod1")]
            s_list = sem("s_list")
            s_row = sem("s_row")
            s_bcast = sem("s_bcast")
            loads = [(c_in, c_t), (conv_w, conv_w_d), (conv_b, conv_b_d), (dt_bias, dt_bias_d),
                     (a_neg, a_log_d), (d_skip, d_skip_d), (norm_w, norm_w_d), (gnorm_w, gnorm_w_d),
                     (w_router, w_router_d), (b_router, b_router_d), (w_in, w_in_d), (w_out, w_out_d)]
            with nc.Block() as block:
                @block.sync
                def _(sp):
                    for dst, src in loads:
                        sp.dma_start(dst[:], src).then_inc(s_load, 16)
                    for a in range(2):
                        if a:
                            sp.wait_ge(s_pe_set, 3)
                        sp.dma_start(w_mod[:].rearrange("p k a n -> p k (a n)"),
                                     w_mod_dh[:, :, a, :]).then_inc(s_wmod[a], 16)
                    sp.wait_ge(s_const, 8)
                    sp.dma_start(env["list_dram"].rearrange("(p n) a -> p (n a)", p=P), zeros[:]).then_inc(s_list, 16)
                    sp.wait_ge(s_setup, 1)
                    sp.dma_start(mod_dram, mod_row[:].rearrange("b m d -> b (m d)")).then_inc(s_row, 16)
                    sp.wait_ge(s_row, 16)
                    for b in range(BATCH):
                        sp.dma_start(mod[:, b, :, :].rearrange("p m d -> p (m d)"),
                                     mod_dram[b:b + 1, 0:5 * DM].broadcast_to([P, 5 * DM])).then_inc(s_bcast, 16)
                    sp.wait_ge(s_bcast, 16 * BATCH)
                    sp.wait_ge(s_list, 16)

                @block.gpsimd
                def _(pool):
                    nc.gpsimd.memset(ident[:], 0.0).then_inc(s_const, 1)
                    nc.gpsimd.memset(tri[:], 1.0).then_inc(s_const, 1)
                    nc.gpsimd.memset(tri_strict[:], 1.0).then_inc(s_const, 1)
                    nc.gpsimd.memset(ones[:], 1.0).then_inc(s_const, 1)
                    nc.gpsimd.memset(starts[:], 1.0).then_inc(s_const, 1)
                    nc.gpsimd.memset(ends[:], 1.0).then_inc(s_const, 1)
                    nc.gpsimd.memset(state[:], 0.0).then_inc(s_const, 1)
                    nc.gpsimd.memset(zeros[:], 0.0).then_inc(s_const, 1)
                    nc.gpsimd.memset(count[:], 0.0).then_inc(s_const, 1)
                    nc.gpsimd.memset(raw[:], 0.0).then_inc(s_const, 1)
                    nc.gpsimd.memset(minus_half[:], -0.5).then_inc(s_const, 1)
                    pool.wait_ge(s_const, 11)
                    nc.gpsimd.affine_select(out=ident[:], in_=ident[:], compare_op=ALU.not_equal, fill=1.0,
                                            base=0, pattern=[[-1, P]], channel_multiplier=1).then_inc(s_const, 1)
                    nc.gpsimd.affine_select(out=tri[:], in_=tri[:], compare_op=ALU.is_ge, fill=0.0,
                                            base=0, pattern=[[1, P]], channel_multiplier=-1).then_inc(s_const, 1)
                    nc.gpsimd.affine_select(out=tri_strict[:], in_=tri_strict[:], compare_op=ALU.is_gt, fill=0.0,
                                            base=0, pattern=[[1, P]], channel_multiplier=-1).then_inc(s_const, 1)
                    nc.gpsimd.memset(starts[:].rearrange("p (b c) -> p b c", b=BATCH)[:, :, 0:1], 0.0).then_inc(s_const, 1)
                    nc.gpsimd.memset(ends[:].rearrange("p (b c) -> p b c", b=BATCH)[:, :, CPB - 1:CPB], 0.0).then_inc(s_const, 1)
                    nc.gpsimd.iota(iota_e[:], [[1, EXPERTS]], base=0, channel_multiplier=0,
                                   allow_small_or_imprecise_dtypes=True).then_inc(s_iota, 1)
                    nc.gpsimd.iota(iota_p[:], [[1, 1]], base=0, channel_multiplier=1,
                                   allow_small_or_imprecise_dtypes=True).then_inc(s_iota, 1)
                    nc.gpsimd.iota(tok_id[:], [[P, 2]], base=-2 * P, channel_multiplier=1,
                                   allow_small_or_imprecise_dtypes=True).then_inc(s_iota, 1)

                @block.scalar
                def _(act):
                    act.wait_ge(s_load, 16 * len(loads))
                    nc.scalar.activation(c_tanh[:], c_in[:], ACT.Tanh, scale=0.5).then_inc(s_act_set, 1)
                    nc.scalar.activation(a_neg[:], a_neg[:], ACT.Exp).then_inc(s_act_set, 1)
                    nc.scalar.mul(norm_w[:], norm_w[:], float(DM) ** 0.5).then_inc(s_act_set, 1)
                    nc.scalar.mul(gnorm_w[:], gnorm_w[:], float(DI) ** 0.5).then_inc(s_act_set, 1)
                    act.wait_ge(s_act_set, 4)
                    for k in range(KD):
                        nc.scalar.activation(w_in[:, k, 0:DIN // 2], w_in[:, k, 0:DIN // 2], ACT.Copy,
                                             scale=norm_w[:, k:k + 1]).then_inc(s_act_set, 1)
                    for k in range(KI):
                        nc.scalar.activation(w_out[:, k, :], w_out[:, k, :], ACT.Copy,
                                             scale=gnorm_w[:, k:k + 1]).then_inc(s_act_set, 1)

                @block.tensor
                def _(pe):
                    pe.wait_ge(s_mod, 2)
                    for m in range(6):
                        if m % 3 == 0:
                            pe.wait_ge(s_wmod[m // 3], 16)
                        for k in range(KD):
                            last = nc.tensor.matmul(half(m)[0:BATCH, :], c_silu[:, k, :], w_mod[:, k, m % 3, :],
                                                    start=(k == 0), stop=(k == KD - 1))
                        last.then_inc(s_pe_set, 1)

                @block.vector
                def _(dve):
                    dve.wait_ge(s_act_set, 1)
                    nc.vector.scalar_tensor_tensor(out=c_silu[:].rearrange("p k b -> p (k b)"),
                                                   in0=c_tanh[:].rearrange("p k b -> p (k b)"), scalar=1.0,
                                                   in1=c_in[:].rearrange("p k b -> p (k b)"),
                                                   op0=ALU.add, op1=ALU.mult).then_inc(s_mod, 1)
                    dve.wait_ge(s_mod, 1)
                    nc.vector.tensor_scalar(c_silu[:], c_silu[:], 0.5, None, ALU.mult).then_inc(s_mod, 1)
                    dve.wait_ge(s_act_set, 4)
                    nc.vector.tensor_scalar(a_neg[:], a_neg[:], -1.0, None, ALU.mult)
                    nc.vector.tensor_scalar(conv_w[:], conv_w[:], 0.5, None, ALU.mult)
                    nc.vector.tensor_scalar(conv_b[:], conv_b[:], 0.5, None, ALU.mult)
                    for k in range(KD):
                        nc.vector.tensor_scalar(w_in[:, k, DIN // 2:DIN], w_in[:, k, DIN // 2:DIN],
                                                norm_w[:, k:k + 1], None, ALU.mult)
                    n = 2
                    for m in range(6):
                        dve.wait_ge(s_pe_set, m + 1)
                        row = mod_row[:, m, :]
                        ps = half(m)[0:BATCH, :]
                        if m % 3 == 0:
                            nc.vector.tensor_copy(row, ps).then_inc(s_mod, 1)
                            n += 1
                        elif m % 3 == 1:
                            nc.vector.tensor_scalar(row, ps, 1.0, None, ALU.add).then_inc(s_mod, 1)
                            n += 1
                        else:
                            nc.vector.tensor_copy(row, ps).then_inc(s_mod, 1)
                            dve.wait_ge(s_mod, n + 1)
                            nc.vector.scalar_tensor_tensor(out=mod_abs[:], in0=row, scalar=-1.0, in1=row,
                                                           op0=ALU.mult, op1=ALU.max).then_inc(s_mod, 1)
                            nc.vector.tensor_scalar(mod_sign[:], row, 0.0, 2.0, ALU.is_ge, ALU.mult).then_inc(s_mod, 1)
                            dve.wait_ge(s_mod, n + 3)
                            nc.vector.tensor_scalar(mod_abs[:], mod_abs[:], 0.25, None, ALU.max).then_inc(s_mod, 1)
                            nc.vector.tensor_scalar(mod_sign[:], mod_sign[:], -1.0, None, ALU.add).then_inc(s_mod, 1)
                            dve.wait_ge(s_mod, n + 5)
                            nc.vector.tensor_tensor(row, mod_abs[:], mod_sign[:], ALU.mult).then_inc(s_mod, 1)
                            n += 6
                    dve.wait_ge(s_mod, n)
                    nc.vector.tensor_copy(mod_abs[:, 0:1], mod_row[:, 0, 0:1]).then_inc(s_setup, 1)

        passed = sem("passed")
        SH_A, SC_A, G_A, SH_B, SC_B = range(5)

        xin = sb("xin", [P, 2, DM])
        st1 = sb("st1", [P, 6])
        mv1 = sb("mv1", [P, 2])
        ve1 = sb("ve1", [P, 1])
        rs1 = sb("rs1", [P, 1])
        nm1 = sb("nm1", [P, 1])
        hn = sb("hn", [P, DM])
        h = sb("h", [P, DM])
        junk = sb("junk", [P, DI], mybir.dt.bfloat16)
        ssq = sb("ssq", [P, 1])
        rre = sb("rre", [P, 1])
        rr = sb("rr", [P, 1])
        xr = sb("xr", [P, DM])
        xg = sb("xg", [P, 2, DM])
        xn_t = sb("xn_t", [P, KD, P])
        acc = sb("acc", [P, NE, P])
        xbc = sb("xbc", [P, 2, NE, P])
        gz = sb("gz", [P, DI])
        sp_x = sb("sp_x", [P, NH])
        sp_a = sb("sp_a", [P, NH])
        sp_u = sb("sp_u", [P, NH])
        sp_r = sb("sp_r", [P, NH])
        sp_s = sb("sp_s", [P, NH])
        sp_q = sb("sp_q", [P, NH])
        sp_p = sb("sp_p", [P, NH])
        sp_m = sb("sp_m", [P, NH])
        dt = sb("dt", [P, NH])
        dta = sb("dta", [P, NH])
        xt = sb("xt", [P, DI])
        btok = sb("btok", [P, P])
        gm = sb("gm", [P, P])
        acs = sb("acs", [P, 3 * NH])
        eacs = sb("eacs", [P, 3 * NH])
        etk = sb("etk", [P, NH])
        x1s = sb("x1s", [P, DI])
        x2s = sb("x2s", [P, DI])
        lm = sb("lm", [P, NH * P])
        tmp_s = sb("tmp_s", [P, DI])
        y = sb("y", [P, DI])
        ssq2 = sb("ssq2", [P, 1])
        r2e = sb("r2e", [P, 1])
        r2 = sb("r2", [P, 1])
        y_t = sb("y_t", [P, KI, P])
        x1 = sb("x1", [P, 2, DM])
        st2 = sb("st2", [P, 6])
        mv2 = sb("mv2", [P, 2])
        ve2 = sb("ve2", [P, 1])
        rs2 = sb("rs2", [P, 1])
        nm2 = sb("nm2", [P, 1])
        hn2 = sb("hn2", [P, DM])
        h2 = sb("h2", [P, 2, DM])
        h2_t = sb("h2_t", [P, KD, P])
        trt = sb("trt", [P, EXPERTS])
        sc = sb("sc", [P, EXPERTS])
        swb = sb("swb", [P, EXPERTS])
        g8 = sb("g8", [P, GROUPS, 8])
        gs = sb("gs", [P, GROUPS])
        gmax = sb("gmax", [P, 8])
        gidx = sb("gidx", [P, 8], U32)
        gidf = sb("gidf", [P, 8])
        gcmp = sb("gcmp", [P, GROUPS, TOPG])
        gmask = sb("gmask", [P, GROUPS])
        ms = sb("ms", [P, EXPERTS])
        emax = sb("emax", [P, 8])
        eidx = sb("eidx", [P, 8], U32)
        eidf = sb("eidf", [P, 8])
        oh = sb("oh", [P, TOPK, EXPERTS])
        ohs = sb("ohs", [P, TOPK, EXPERTS])
        picked = sb("picked", [P, EXPERTS])
        wk = sb("wk", [P, TOPK])
        wsum = sb("wsum", [P, 1])
        winv = sb("winv", [P, 1])
        rank = sb("rank", [P, EXPERTS])
        rk = sb("rk", [P, TOPK])
        pos = sb("pos", [P, 2, TOPK], I32)

        x_in = [sem("x_in0"), sem("x_in1")]
        x1_st = [sem("x1_st0"), sem("x1_st1")]
        h2_st = [sem("h2_st0"), sem("h2_st1")]
        list_st = [sem("list_st0"), sem("list_st1")]
        names = ("ln1_stat hn_done h_half h_done ssq_done rr_done xr_done xg_half xg_done "
                 "xnT_ps xnT_sb xbc_ps raw_sb carry conv_done conv_th xbc_done dt_raw dt_abs dt_u dt_done "
                 "z_ps z_th gz_done xtok_ps xt_sb small_ps small_sb exps btok_sb etk_done rows_ps seg_done "
                 "l_exp m_done x1s_done x2s_done tmps_done xd_done yoff_ps yoff_sb states_ps state_done "
                 "ydiag_ps yadd_done y_done ssq2_done r2_done yn_done yT_ps yT_sb out_ps x1_done ln2_stat "
                 "hn2_done h2_half h2_done h2T_ps h2T_sb rt_ps rt_th sc_done picked_done rank_ps rank_done pos_done "
                 "dve_sp ln1_var ln1_rs ln2_var ln2_rs rr_var r2_var dve_e dve_f dve_b dve_t1 dve_t2 dve_l").split()
        S = {n: sem(n) for n in names}

        def modrow(which, chunk):
            b = chunk // CPB
            if isinstance(chunk, int):
                return mod[:, b, which, :]
            return mod[:].rearrange("p b m d -> p (b m d)")[:, bass.ds(b * (5 * DM) + which * DM, DM)]

        def col(t, chunk):
            if isinstance(chunk, int):
                return t[:, chunk:chunk + 1]
            return t[:, bass.ds(chunk, 1)]

        def rows_of(dram, chunk):
            if isinstance(chunk, int):
                return dram[chunk * P:(chunk + 1) * P, :]
            return dram[bass.ds(chunk * P, P), :]

        def topk_at(t, chunk):
            flat = t[:].rearrange("p n k -> p (n k)")
            if isinstance(chunk, int):
                return flat[:, chunk * TOPK:(chunk + 1) * TOPK]
            return flat[:, bass.ds(chunk * TOPK, TOPK)]

        def heads(t, n=NH, w=HD):
            return t.rearrange("p (h w) -> p h w", h=n)

        def per_head(t, w=HD):
            return t.unsqueeze(2).to_broadcast([P, t.shape[1], w])

        def steps(eng, step):
            def one(s):
                step(*(v if 0 <= v < NCH else None for v in (s + 2, s + 1, s, s - 1, s - 2)), s % 2)
            for s in range(-2, 2):
                one(s)
            with eng.Fori(2, NCH - 5, 2) as s:
                for p in range(2):
                    v = s + p
                    step(v + 2, v + 1, v, v - 1, v - 2, p)
            for s in range(NCH - 4, NCH + 2):
                one(s)

        with nc.Block() as block:
            @block.sync
            def _(sp):
                for e in range(2):
                    sp.dma_start(xin[:, e, :], rows_of(x, e)).then_inc(x_in[e], 16)

                def step(e, f, c, t, q, p):
                    if e is not None and not (isinstance(e, int) and (e == 0 or e >= NCH - 1)):
                        sp.wait_ge(S["xg_done"], e)
                        sp.dma_start(xin[:, 1 - p, :], rows_of(x, e + 1)).then_inc(x_in[1 - p], 16)
                    if t is not None:
                        sp.wait_ge(S["h2_done"], t + 1)
                        sp.dma_start(rows_of(h2_dram, t), h2[:, 1 - p, :]).then_inc(h2_st[1 - p], 16)
                    if c is not None:
                        sp.wait_ge(S["x1_done"], c + 1)
                        sp.dma_start(rows_of(x1_dram, c), x1[:, p, :]).then_inc(x1_st[p], 16)

                steps(sp, step)
                for p in range(2):
                    sp.wait_ge(x1_st[p], 16 * NCH // 2)
                    sp.wait_ge(h2_st[p], 16 * NCH // 2)

            @block.gpsimd
            def _(pool):
                def step(e, f, c, t, q, p):
                    if t is not None:
                        pool.wait_ge(S["ln2_var"], t + 1)
                        at_least(pool, S["hn2_done"], t)
                        nc.gpsimd.tensor_tensor(rs2[:], ve2[:], minus_half[:], ALU.pow).then_inc(S["ln2_rs"], 1)
                        wait_apart(pool, S["ln2_rs"], t + 1, passed)
                        nc.gpsimd.tensor_scalar(nm2[:], mv2[:, 0:1], rs2[:], -1.0, ALU.mult, ALU.mult).then_inc(S["ln2_stat"], 1)
                        pool.wait_ge(S["hn2_done"], t + 1)
                        at_least(pool, h2_st[1 - p], 16 * (t // 2))
                        at_least(pool, S["h2T_ps"], t - 1)
                        nc.gpsimd.tensor_tensor(h2[:, 1 - p, :], hn2[:], modrow(SC_B, t), ALU.mult).then_inc(S["h2_half"], 1)
                        pool.wait_ge(S["h2_half"], t + 1)
                        nc.gpsimd.tensor_tensor(h2[:, 1 - p, :], h2[:, 1 - p, :], modrow(SH_B, t), ALU.add).then_inc(S["h2_done"], 1)
                    if e is not None:
                        pool.wait_ge(S["ln1_var"], e + 1)
                        at_least(pool, S["hn_done"], e)
                        nc.gpsimd.tensor_tensor(rs1[:], ve1[:], minus_half[:], ALU.pow).then_inc(S["ln1_rs"], 1)
                        wait_apart(pool, S["ln1_rs"], e + 1, passed)
                        nc.gpsimd.tensor_scalar(nm1[:], mv1[:, 0:1], rs1[:], -1.0, ALU.mult, ALU.mult).then_inc(S["ln1_stat"], 1)
                        pool.wait_ge(S["hn_done"], e + 1)
                        at_least(pool, S["xr_done"], e)
                        nc.gpsimd.tensor_tensor(h[:], hn[:], modrow(SC_A, e), ALU.mult).then_inc(S["h_half"], 1)
                        pool.wait_ge(S["h_half"], e + 1)
                        nc.gpsimd.tensor_tensor(h[:], h[:], modrow(SH_A, e), ALU.add).then_inc(S["h_done"], 1)
                        wait_apart(pool, S["ssq_done"], e + 1, passed)
                        nc.gpsimd.tensor_scalar(rre[:], ssq[:], DM * LN_EPS, None, ALU.add).then_inc(S["rr_var"], 1)
                        pool.wait_ge(S["rr_var"], e + 1)
                        nc.gpsimd.tensor_tensor(rr[:], rre[:], minus_half[:], ALU.pow).then_inc(S["rr_done"], 1)
                    if q is not None:
                        wait_apart(pool, S["pos_done"], q + 1, passed)
                        for k in range(TOPK):
                            pool.indirect_dma_start(
                                list_dram, bass.IndirectOffsetOnAxis(ap=pos[:, p, k:k + 1], axis=0),
                                tok_id[:, p:p + 1], None).then_inc(list_st[p], 16)
                    if c is not None:
                        pool.wait_ge(S["x1s_done"], c + 1)
                        pool.wait_ge(S["exps"], c + 1)
                        at_least(pool, S["states_ps"], c)
                        nc.gpsimd.tensor_tensor(heads(x2s[:]), heads(x1s[:]), per_head(eacs[:, 2 * NH:3 * NH]),
                                                ALU.mult).then_inc(S["x2s_done"], 1)
                        pool.wait_ge(S["etk_done"], c + 1)
                        at_least(pool, S["state_done"], c)
                        nc.gpsimd.tensor_tensor(heads(tmp_s[:]), heads(state[:]), per_head(etk[:]),
                                                ALU.mult).then_inc(S["tmps_done"], 1)
                        nc.gpsimd.tensor_tensor(heads(xt[:]), heads(xt[:]), per_head(d_skip[:]),
                                                ALU.mult).then_inc(S["xd_done"], 1)
                        wait_apart(pool, S["ssq2_done"], c + 1, passed)
                        nc.gpsimd.tensor_scalar(r2e[:], ssq2[:], 4 * DI * LN_EPS, None, ALU.add).then_inc(S["r2_var"], 1)
                        pool.wait_ge(S["r2_var"], c + 1)
                        at_least(pool, S["yn_done"], c)
                        nc.gpsimd.tensor_tensor(r2[:], r2e[:], minus_half[:], ALU.pow).then_inc(S["r2_done"], 1)
                    if e is not None:
                        at_least(pool, S["x1_done"], e - 1)
                        pool.wait_ge(S["h_done"], e + 1)
                        nc.gpsimd.tensor_tensor(xg[:, p, :], h[:], modrow(G_A, e), ALU.mult).then_inc(S["xg_half"], 1)
                        pool.wait_ge(S["xg_half"], e + 1)
                        pool.wait_ge(x_in[p], 16 * (e // 2 + 1))
                        nc.gpsimd.tensor_tensor(xg[:, p, :], xg[:, p, :], xin[:, p, :], ALU.add).then_inc(S["xg_done"], 1)

                steps(pool, step)
                for p in range(2):
                    pool.wait_ge(list_st[p], 16 * TOPK * NCH // 2)

            @block.scalar
            def _(act):
                def step(e, f, c, t, q, p):
                    if t is not None:
                        act.wait_ge(S["ln2_stat"], t + 1)
                        at_least(act, S["h2_done"], t)
                        nc.scalar.activation(hn2[:], x1[:, 1 - p, :], ACT.Identity, bias=nm2[:], scale=rs2[:]).then_inc(S["hn2_done"], 1)
                    if c is not None:
                        act.wait_ge(S["xtok_ps"], c + 1)
                        at_least(act, S["x1s_done"], c)
                        at_least(act, S["yadd_done"], c)
                        nc.scalar.copy(xt[:], bank[1][:]).then_inc(S["xt_sb"], 1)
                        act.wait_ge(S["small_sb"], c + 1)
                        at_least(act, S["yoff_sb"], c)
                        at_least(act, S["x2s_done"], c)
                        nc.scalar.activation(eacs[:], acs[:], ACT.Exp).then_inc(S["exps"], 1)
                        at_least(act, S["states_ps"], c)
                        nc.scalar.activation(btok[:], half(4)[:, P:2 * P], ACT.Copy, scale=col(ends, c)).then_inc(S["btok_sb"], 1)
                    if e is not None:
                        act.wait_ge(S["ln1_stat"], e + 1)
                        at_least(act, S["h_done"], e)
                        nc.scalar.activation(hn[:], xin[:, p, :], ACT.Identity, bias=nm1[:], scale=rs1[:]).then_inc(S["hn_done"], 1)
                    if f is not None:
                        act.wait_ge(S["xnT_ps"], f + 1)
                        at_least(act, S["z_ps"], 2 * f)
                        nc.scalar.copy(xn_t[:].rearrange("p k t -> p (k t)"), half(0)).then_inc(S["xnT_sb"], 1)
                    if c is not None:
                        for j in range(2):
                            act.wait_ge(S["seg_done"], 2 * c + j + 1)
                            nc.scalar.activation(lm[:, j * DI:(j + 1) * DI], lm[:, j * DI:(j + 1) * DI], ACT.Exp).then_inc(S["l_exp"], 1)
                    if e is not None:
                        act.wait_ge(S["h_done"], e + 1)
                        at_least(act, S["rr_done"], e)
                        nc.scalar.activation(junk[:, 0:DM], h[:], ACT.Square, accum_out=ssq[:]).then_inc(S["ssq_done"], 1)
                    if f is not None:
                        act.wait_ge(S["carry"], f + 1)
                        for g in range(3):
                            act.wait_ge(S["xbc_ps"], 3 * f + g + 1)
                            n = (4, 4, 2)[g]
                            nc.scalar.copy(raw[:, 1 - p, 4 * g:4 * g + n, TAPS - 1:],
                                           half(1 - g % 2)[:, 0:n * P].rearrange("p (n t) -> p n t", n=n)).then_inc(S["raw_sb"], 1)
                    if e is not None:
                        act.wait_ge(S["rr_done"], e + 1)
                        at_least(act, S["xnT_ps"], e)
                        nc.scalar.activation(xr[:], h[:], ACT.Copy, scale=rr[:]).then_inc(S["xr_done"], 1)
                    if t is not None:
                        act.wait_ge(S["h2T_ps"], t + 1)
                        at_least(act, S["rt_ps"], t)
                        nc.scalar.copy(h2_t[:].rearrange("p k t -> p (k t)"), half(5)).then_inc(S["h2T_sb"], 1)
                    if f is not None:
                        act.wait_ge(S["conv_done"], f + 1)
                        at_least(act, S["yoff_ps"], f - 1)
                        nc.scalar.activation(xbc[:, 1 - p, :, :], acc[:], ACT.Tanh).then_inc(S["conv_th"], 1)
                    if t is not None:
                        act.wait_ge(S["rt_ps"], t + 1)
                        at_least(act, S["sc_done"], t)
                        nc.scalar.activation(trt[:], half(6)[:, 0:EXPERTS], ACT.Tanh, scale=0.5).then_inc(S["rt_th"], 1)
                    if f is not None:
                        act.wait_ge(S["z_ps"], 2 * f + 1)
                        at_least(act, S["y_done"], f)
                        nc.scalar.activation(gz[:, 0:512], half(0), ACT.Tanh, scale=0.5).then_inc(S["z_th"], 1)
                    if c is not None:
                        act.wait_ge(S["y_done"], c + 1)
                        at_least(act, S["r2_done"], c)
                        nc.scalar.activation(junk[:], y[:], ACT.Square, accum_out=ssq2[:]).then_inc(S["ssq2_done"], 1)
                    if f is not None:
                        act.wait_ge(S["dt_abs"], f + 1)
                        nc.scalar.activation(sp_u[:], sp_a[:], ACT.Exp, scale=-1.0).then_inc(S["dt_u"], 1)
                        act.wait_ge(S["z_ps"], 2 * f + 2)
                        nc.scalar.activation(gz[:, 512:1024], half(1), ACT.Tanh, scale=0.5).then_inc(S["z_th"], 1)
                    if c is not None:
                        act.wait_ge(S["r2_done"], c + 1)
                        nc.scalar.activation(y[:], y[:], ACT.Copy, scale=r2[:]).then_inc(S["yn_done"], 1)
                        act.wait_ge(S["yT_ps"], c + 1)
                        at_least(act, S["out_ps"], c)
                        nc.scalar.copy(y_t[:].rearrange("p k t -> p (k t)"), bank[2][:]).then_inc(S["yT_sb"], 1)

                steps(act, step)

            @block.tensor
            def _(pe):
                def step(e, f, c, t, q, p):
                    if c is not None:
                        pe.wait_ge(S["xbc_done"], c + 1)
                        at_least(pe, S["rank_done"], c - 1)
                        at_least(pe, S["yadd_done"], c)
                        for i in range(KI):
                            last = nc.tensor.transpose(bank[1][:, i * P:(i + 1) * P], xbc[:, p, i, :], ident[:])
                        last.then_inc(S["xtok_ps"], 1)
                        at_least(pe, S["yT_sb"], c)
                        pe.wait_ge(S["dt_done"], c + 1)
                        nc.tensor.matmul(half(4)[:, 0:P], xbc[:, p, 8, :], xbc[:, p, 9, :], start=True, stop=True)
                        nc.tensor.transpose(half(4)[:, P:2 * P], xbc[:, p, 8, :], ident[:])
                        nc.tensor.matmul(half(4)[:, 2 * P:2 * P + NH], tri[:], dta[:], start=True, stop=True)
                        nc.tensor.matmul(half(4)[:, 2 * P + NH:2 * P + 2 * NH], ones[:], dta[:], start=True, stop=True).then_inc(S["small_ps"], 1)
                        at_least(pe, S["x1_done"], c)
                        at_least(pe, S["rt_th"], c - 1)
                        for j in range(2):
                            if j == 1:
                                pe.wait_ge(S["xt_sb"], c + 1)
                            dst = bank[3] if j == 0 else bank[1]
                            for i in range(8):
                                hh = 8 * j + i
                                last = nc.tensor.matmul(dst[:, i * P:(i + 1) * P], dta[:, hh:hh + 1].to_broadcast([P, P]),
                                                        tri[:], start=True, stop=True)
                            last.then_inc(S["rows_ps"], 1)
                    if f is not None:
                        pe.wait_ge(S["xr_done"], f + 1)
                        at_least(pe, S["gz_done"], 2 * f - 1)
                        for k in range(KD):
                            last = nc.tensor.transpose(half(0)[:, k * P:(k + 1) * P], xr[:, k * P:(k + 1) * P], ident[:])
                        last.then_inc(S["xnT_ps"], 1)
                        pe.wait_ge(S["xnT_sb"], f + 1)
                        at_least(pe, S["gz_done"], 2 * f)
                        for g in range(3):
                            if g == 2:
                                pe.wait_ge(S["raw_sb"], 3 * f + 1)
                            for i in range((4, 4, 2)[g]):
                                m = DI + (4 * g + i) * P
                                for k in range(KD):
                                    last = nc.tensor.matmul(half(1 - g % 2)[:, i * P:(i + 1) * P], w_in[:, k, m:m + P],
                                                            xn_t[:, k, :], start=(k == 0), stop=(k == KD - 1))
                            if g == 2:
                                for k in range(KD):
                                    last = nc.tensor.matmul(half(1)[:, 2 * P:2 * P + NH], xn_t[:, k, :],
                                                            w_in[:, k, DIN - NH:DIN], start=(k == 0), stop=(k == KD - 1))
                            last.then_inc(S["xbc_ps"], 1)
                    if t is not None:
                        pe.wait_ge(S["h2_done"], t + 1)
                        pe.wait_ge(S["yT_sb"], t + 1)
                        for k in range(KD):
                            last = nc.tensor.transpose(half(5)[:, k * P:(k + 1) * P], h2[:, 1 - p, k * P:(k + 1) * P], ident[:])
                        last.then_inc(S["h2T_ps"], 1)
                    if c is not None:
                        pe.wait_ge(S["seg_done"], 2 * c + 1)
                        at_least(pe, S["state_done"], c)
                        for j in range(2):
                            last = nc.tensor.matmul(bank[3][:, j * 512:(j + 1) * 512], xbc[:, p, 9, :],
                                                    state[:, j * 512:(j + 1) * 512], start=True, stop=True)
                        last.then_inc(S["yoff_ps"], 1)
                        pe.wait_ge(S["btok_sb"], c + 1)
                        pe.wait_ge(S["small_sb"], c + 1)
                        at_least(pe, S["h2T_sb"], c)
                        pe.wait_ge(S["x2s_done"], c + 1)
                        for j in range(2):
                            last = nc.tensor.matmul(bank[2][:, j * 512:(j + 1) * 512], btok[:],
                                                    x2s[:, j * 512:(j + 1) * 512], start=True, stop=True)
                        last.then_inc(S["states_ps"], 1)
                        pe.wait_ge(S["x1s_done"], c + 1)
                        pe.wait_ge(S["m_done"], 2 * c + 2)
                        for hh in range(NH):
                            last = nc.tensor.matmul(bank[1][:, hh * HD:(hh + 1) * HD], lm[:, hh * P:(hh + 1) * P],
                                                    x1s[:, hh * HD:(hh + 1) * HD], start=True, stop=True)
                        last.then_inc(S["ydiag_ps"], 1)
                    if t is not None:
                        pe.wait_ge(S["h2T_sb"], t + 1)
                        if c is not None:
                            pe.wait_ge(S["yoff_sb"], c + 1)
                        for k in range(KD):
                            last = nc.tensor.matmul(half(6)[:, 0:EXPERTS], h2_t[:, k, :], w_router[:, k, :],
                                                    start=(k == 0), stop=(k == KD - 1))
                        last.then_inc(S["rt_ps"], 1)
                    if f is not None:
                        for j in range(2):
                            pe.wait_ge(S["raw_sb"], 3 * f + 2 + j)
                            if j == 1:
                                pe.wait_ge(S["dt_raw"], f + 1)
                            for k in range(KD):
                                last = nc.tensor.matmul(half(j), xn_t[:, k, :], w_in[:, k, j * 512:(j + 1) * 512],
                                                        start=(k == 0), stop=(k == KD - 1))
                            last.then_inc(S["z_ps"], 1)
                    if c is not None:
                        pe.wait_ge(S["yn_done"], c + 1)
                        pe.wait_ge(S["state_done"], c + 1)
                        for i in range(KI):
                            last = nc.tensor.transpose(bank[2][:, i * P:(i + 1) * P], y[:, i * P:(i + 1) * P], ident[:])
                        last.then_inc(S["yT_ps"], 1)
                    if t is not None:
                        pe.wait_ge(S["picked_done"], t + 1)
                        if c is not None:
                            pe.wait_ge(S["yadd_done"], c + 1)
                        nc.tensor.matmul(half(2)[:, 0:EXPERTS], tri_strict[:], picked[:], start=True, stop=True)
                        nc.tensor.matmul(half(2)[:, EXPERTS:2 * EXPERTS], ones[:], picked[:], start=True, stop=True).then_inc(S["rank_ps"], 1)
                    if c is not None:
                        pe.wait_ge(S["yT_sb"], c + 1)
                        pe.wait_ge(S["yoff_sb"], c + 1)
                        for i in range(KI):
                            last = nc.tensor.matmul(half(7), y_t[:, i, :], w_out[:, i, :], start=(i == 0), stop=(i == KI - 1))
                        last.then_inc(S["out_ps"], 1)

                steps(pe, step)

            @block.vector
            def _(dve):
                early = Order(dve, S["dve_e"], 2)
                softplus = Order(dve, S["dve_f"], 11)
                conv = Order(dve, S["dve_l"], 2 * TAPS - 1)
                back = Order(dve, S["dve_b"], 5)
                route = Order(dve, S["dve_t1"], 15)
                place = Order(dve, S["dve_t2"], 5)
                tt, ts, stt = nc.vector.tensor_tensor, nc.vector.tensor_scalar, nc.vector.scalar_tensor_tensor

                def step(e, f, c, t, q, p):
                    if c is not None:
                        back.begin(c)
                        dve.wait_ge(S["small_ps"], c + 1)
                        tt(gm[:], half(4)[:, 0:P], tri[:], ALU.mult)
                        at_least(dve, S["exps"], c)
                        back.mark(nc.vector.tensor_copy(acs[:, 0:2 * NH], half(4)[:, 2 * P:2 * P + 2 * NH]))
                        back.wait()
                        tt(acs[:, 2 * NH:3 * NH], acs[:, NH:2 * NH], acs[:, 0:NH], ALU.subtract).then_inc(S["small_sb"], 1)
                    if e is not None:
                        early.begin(e)
                        dve.wait_ge(x_in[p], 16 * (e // 2 + 1))
                        early.mark(nc.vector.bn_stats(st1[:], xin[:, p, :]))
                        at_least(dve, S["ln1_stat"], e)
                        early.wait_apart(passed)
                        early.mark(nc.vector.bn_aggr(mv1[:], st1[:]))
                        early.wait()
                        ts(ve1[:], mv1[:, 1:2], LN_EPS, None, ALU.add).then_inc(S["ln1_var"], 1)
                        early.end()
                    if f is not None:
                        at_least(dve, S["raw_sb"], 3 * f)
                        ts(raw[:, 1 - p, :, 0:TAPS - 1], raw[:, p, :, P:P + TAPS - 1], col(starts, f), None,
                           ALU.mult).then_inc(S["carry"], 1)
                    if c is not None:
                        dve.wait_ge(S["exps"], c + 1)
                        at_least(dve, S["tmps_done"], c)
                        ts(etk[:], eacs[:, NH:2 * NH], col(ends, c), None, ALU.mult).then_inc(S["etk_done"], 1)
                        at_least(dve, S["ydiag_ps"], c)
                        dve.wait_ge(S["small_sb"], c + 1)
                        for j in range(2):
                            dve.wait_ge(S["rows_ps"], 2 * c + j + 1)
                            for i in range(8):
                                hh = 8 * j + i
                                last = ts(lm[:, hh * P:(hh + 1) * P], (bank[3] if j == 0 else bank[1])[:, i * P:(i + 1) * P],
                                          acs[:, hh:hh + 1], 0.0, ALU.subtract, ALU.min)
                            last.then_inc(S["seg_done"], 1)
                        dve.wait_ge(S["xt_sb"], c + 1)
                        dve.wait_ge(S["dt_done"], c + 1)
                        at_least(dve, S["x2s_done"], c)
                        tt(heads(x1s[:]), heads(xt[:]), per_head(dt[:]), ALU.mult).then_inc(S["x1s_done"], 1)
                    if c is not None:
                        for j in range(2):
                            dve.wait_ge(S["l_exp"], 2 * c + j + 1)
                            tt(heads(lm[:, j * DI:(j + 1) * DI], 8, P), heads(lm[:, j * DI:(j + 1) * DI], 8, P),
                               gm[:].unsqueeze(1).to_broadcast([P, 8, P]), ALU.mult).then_inc(S["m_done"], 1)
                    if f is not None:
                        conv.begin(f)
                        dve.wait_ge(S["raw_sb"], 3 * f + 3)
                        dve.wait_ge(S["carry"], f + 1)
                        for k in range(TAPS):
                            for hf in range(2):
                                if k:
                                    conv.wait(2 * (k - 1) + hf + 1)
                                for i in range(5 * hf, 5 * hf + 5):
                                    src = raw[:, 1 - p, i, k:k + P]
                                    if k == 0:
                                        last = ts(acc[:, i, :], src, conv_w[:, i, 0:1], conv_b[:, i:i + 1], ALU.mult, ALU.add)
                                    else:
                                        last = stt(out=acc[:, i, :], in0=src, scalar=conv_w[:, i, k:k + 1],
                                                   in1=acc[:, i, :], op0=ALU.mult, op1=ALU.add)
                                if (k, hf) == (TAPS - 1, 1):
                                    last.then_inc(S["conv_done"], 1)
                                else:
                                    conv.mark(last)
                        conv.end()
                    if c is not None:
                        dve.wait_ge(S["yoff_ps"], c + 1)
                        at_least(dve, S["yT_ps"], c)
                        tt(heads(y[:]), heads(bank[3][:]), per_head(eacs[:, 0:NH]), ALU.mult).then_inc(S["yoff_sb"], 1)
                        dve.wait_ge(S["states_ps"], c + 1)
                        dve.wait_ge(S["tmps_done"], c + 1)
                        tt(state[:], tmp_s[:], bank[2][:], ALU.add).then_inc(S["state_done"], 1)
                    if f is not None:
                        dve.wait_ge(S["conv_th"], f + 1)
                        stt(out=xbc[:, 1 - p, :, :].rearrange("p n t -> p (n t)"), in0=xbc[:, 1 - p, :, :].rearrange("p n t -> p (n t)"),
                            scalar=1.0, in1=acc[:].rearrange("p n t -> p (n t)"), op0=ALU.add, op1=ALU.mult).then_inc(S["xbc_done"], 1)
                    if c is not None:
                        dve.wait_ge(S["ydiag_ps"], c + 1)
                        dve.wait_ge(S["yoff_sb"], c + 1)
                        back.mark(tt(y[:], y[:], bank[1][:], ALU.add))
                        back.wait()
                        dve.wait_ge(S["xd_done"], c + 1)
                        tt(y[:], y[:], xt[:], ALU.add).then_inc(S["yadd_done"], 1)
                        dve.wait_ge(S["yadd_done"], c + 1)
                        dve.wait_ge(S["gz_done"], 2 * c + 2)
                        tt(y[:], y[:], gz[:], ALU.mult).then_inc(S["y_done"], 1)
                    if f is not None:
                        softplus.begin(f)
                        dve.wait_ge(S["xbc_ps"], 3 * f + 3)
                        tt(sp_x[:], half(1)[:, 2 * P:2 * P + NH], dt_bias[:], ALU.add).then_inc(S["dt_raw"], 1)
                        dve.wait_ge(S["dt_raw"], f + 1)
                        stt(out=sp_a[:], in0=sp_x[:], scalar=-1.0, in1=sp_x[:], op0=ALU.mult, op1=ALU.max).then_inc(S["dt_abs"], 1)
                    if t is not None:
                        route.begin(t)
                        dve.wait_ge(S["rt_th"], t + 1)
                        ts(sc[:], trt[:], 0.5, 0.5, ALU.mult, ALU.add).then_inc(S["sc_done"], 1)
                        dve.wait_ge(S["sc_done"], t + 1)
                        route.mark(tt(swb[:], sc[:], b_router[:], ALU.add))
                        route.wait_apart(passed)
                        for g in range(GROUPS):
                            last = nc.vector.max(out=g8[:, g, :], in_=swb[:, 8 * g:8 * g + 8])
                        route.mark(last)
                        route.wait()
                        route.mark(tt(gs[:], g8[:, :, 0], g8[:, :, 1], ALU.add))
                        route.wait_apart(passed)
                        route.mark(nc.vector.max(out=gmax[:], in_=gs[:]))
                        route.wait_apart(passed)
                        route.mark(nc.vector.max_index(out=gidx[:], in_max=gmax[:], in_values=gs[:]))
                        route.wait()
                        route.mark(nc.vector.tensor_copy(gidf[:], gidx[:]))
                        route.wait()
                        route.mark(tt(gcmp[:], iota_e[:, 0:GROUPS].unsqueeze(2).to_broadcast([P, GROUPS, TOPG]),
                                      gidf[:, 0:TOPG].unsqueeze(1).to_broadcast([P, GROUPS, TOPG]), ALU.is_equal))
                        route.wait()
                        route.mark(nc.vector.tensor_reduce(gmask[:], gcmp[:], AX.X, ALU.max))
                        route.wait()
                        route.mark(tt(heads(ms[:], GROUPS, 8), heads(swb[:], GROUPS, 8), per_head(gmask[:], 8), ALU.mult))
                        route.wait_apart(passed)
                        route.mark(nc.vector.max(out=emax[:], in_=ms[:]))
                        route.wait_apart(passed)
                        route.mark(nc.vector.max_index(out=eidx[:], in_max=emax[:], in_values=ms[:]))
                        route.wait()
                        route.mark(nc.vector.tensor_copy(eidf[:], eidx[:]))
                        route.wait()
                        route.mark(tt(oh[:], iota_e[:].unsqueeze(1).to_broadcast([P, TOPK, EXPERTS]),
                                      eidf[:].unsqueeze(2).to_broadcast([P, TOPK, EXPERTS]), ALU.is_equal))
                        nc.vector.tensor_copy(topk_at(top_e, t), eidf[:])
                        route.wait()
                        nc.vector.tensor_reduce(picked[:], oh[:].rearrange("p k e -> p e k"), AX.X, ALU.add).then_inc(S["picked_done"], 1)
                        route.mark(tt(ohs[:], oh[:], sc[:].unsqueeze(1).to_broadcast([P, TOPK, EXPERTS]), ALU.mult))
                        route.wait()
                        route.mark(nc.vector.tensor_reduce(wk[:], ohs[:], AX.X, ALU.add))
                        route.end()
                    if f is not None:
                        dve.wait_ge(S["dt_u"], f + 1)
                        softplus.mark(ts(sp_r[:], sp_u[:], 2.0, None, ALU.add))
                        softplus.wait()
                        softplus.mark(nc.vector.reciprocal(sp_r[:], sp_r[:]))
                        softplus.wait()
                        softplus.mark(tt(sp_s[:], sp_u[:], sp_r[:], ALU.mult))
                        softplus.wait()
                        softplus.mark(tt(sp_q[:], sp_s[:], sp_s[:], ALU.mult))
                        softplus.wait()
                        softplus.mark(ts(sp_p[:], sp_q[:], 1.0 / 15, 1.0 / 13, ALU.mult, ALU.add))
                        softplus.wait()
                        src = sp_p
                        softplus.mark(tt(sp_p[:], sp_p[:], sp_q[:], ALU.mult))
                        softplus.wait()
                        for i, d in enumerate((11, 9, 7)):
                            softplus.mark(stt(out=sp_p[:], in0=sp_p[:], scalar=1.0 / d, in1=sp_q[:], op0=ALU.add, op1=ALU.mult))
                            softplus.wait()
                        softplus.mark(stt(out=sp_p[:], in0=sp_p[:], scalar=1.0 / 5, in1=sp_q[:], op0=ALU.add, op1=ALU.mult))
                        softplus.wait()
                    if t is not None:
                        place.begin(t)
                        route.wait(15)
                        place.mark(nc.vector.tensor_reduce(wsum[:], wk[:], AX.X, ALU.add))
                        place.wait()
                        place.mark(ts(winv[:], wsum[:], 1e-20, None, ALU.add))
                        place.wait()
                        place.mark(nc.vector.reciprocal(winv[:], winv[:]))
                        place.wait()
                        ts(topk_at(top_w, t), wk[:], winv[:], 0.5 * ROUTED_SCALE, ALU.mult, ALU.mult)
                    if f is not None:
                        softplus.mark(stt(out=sp_p[:], in0=sp_p[:], scalar=1.0 / 3, in1=sp_q[:], op0=ALU.add, op1=ALU.mult))
                        softplus.wait()
                        softplus.end()
                        stt(out=sp_m[:], in0=sp_p[:], scalar=1.0, in1=sp_s[:], op0=ALU.add, op1=ALU.mult)
                        ts(sp_r[:], sp_x[:], 0.0, None, ALU.max).then_inc(S["dve_sp"], 1)
                        dve.wait_ge(S["dve_sp"], 2 * f + 1)
                        stt(out=dt[:], in0=sp_m[:], scalar=2.0, in1=sp_r[:], op0=ALU.mult, op1=ALU.add).then_inc(S["dve_sp"], 1)
                        dve.wait_ge(S["dve_sp"], 2 * f + 2)
                        at_least(dve, S["rows_ps"], 2 * f)
                        tt(dta[:], dt[:], a_neg[:], ALU.mult).then_inc(S["dt_done"], 1)
                        for j in range(2):
                            dve.wait_ge(S["z_th"], 2 * f + j + 1)
                            stt(out=gz[:, j * 512:(j + 1) * 512], in0=gz[:, j * 512:(j + 1) * 512], scalar=1.0,
                                in1=half(j), op0=ALU.add, op1=ALU.mult).then_inc(S["gz_done"], 1)
                    if t is not None:
                        dve.wait_ge(S["rank_ps"], t + 1)
                        tt(rank[:], half(2)[:, 0:EXPERTS], count[:], ALU.add)
                        tt(count[:], count[:], half(2)[:, EXPERTS:2 * EXPERTS], ALU.add).then_inc(S["rank_done"], 1)
                        at_least(dve, list_st[1 - p], 16 * TOPK * (t // 2))
                        ts(tok_id[:, 1 - p:2 - p], tok_id[:, 1 - p:2 - p], 2.0 * P, None, ALU.add)
                        dve.wait_ge(S["rank_done"], t + 1)
                        place.mark(tt(ohs[:], oh[:], rank[:].unsqueeze(1).to_broadcast([P, TOPK, EXPERTS]), ALU.mult))
                        place.wait()
                        place.mark(nc.vector.tensor_reduce(rk[:], ohs[:], AX.X, ALU.add))
                        place.wait()
                        place.end()
                        nc.vector.tensor_copy(topk_at(top_r, t), rk[:])
                        stt(out=pos[:, 1 - p, :], in0=eidf[:], scalar=float(SEG), in1=rk[:],
                            op0=ALU.mult, op1=ALU.add).then_inc(S["pos_done"], 1)
                    if c is not None:
                        dve.wait_ge(S["out_ps"], c + 1)
                        dve.wait_ge(S["xg_done"], c + 1)
                        at_least(dve, x1_st[p], 16 * (c // 2))
                        at_least(dve, S["hn2_done"], c - 1)
                        back.mark(tt(x1[:, p, :], half(7), modrow(G_A, c), ALU.mult))
                        back.wait()
                        tt(x1[:, p, :], x1[:, p, :], xg[:, p, :], ALU.add).then_inc(S["x1_done"], 1)
                        dve.wait_ge(S["x1_done"], c + 1)
                        back.mark(nc.vector.bn_stats(st2[:], x1[:, p, :]))
                        at_least(dve, S["ln2_stat"], c)
                        back.wait_apart(passed)
                        back.mark(nc.vector.bn_aggr(mv2[:], st2[:]))
                        back.wait()
                        back.end()
                        ts(ve2[:], mv2[:, 1:2], LN_EPS, None, ALU.add).then_inc(S["ln2_var"], 1)

                steps(dve, step)


def tables(nc, top, sem, tile, bank, half, env):
    ident, tri, tri_strict, ones, count = (env[k] for k in ("ident", "tri", "tri_strict", "ones", "count"))
    NB2 = NBLK // 2
    E = EXPERTS
    idx = tile(top, "idx", [P, LCOLS], I32)
    tab_e = tile(top, "tab_e", [1, NBLK], I32)
    tab_col = tile(top, "tab_col", [1, NBLK], I32)
    tab_end = tile(top, "tab_end", [1, E], I32)
    base = tile(top, "base", [P, E])
    out_rows = tile(top, "out_rows", [P, NCH * TOPK], I32)
    rows = env["list_dram"].rearrange("(r n) a -> r (n a)", n=P)
    full = LCOLS // P
    rest = LCOLS - full * P

    with ExitStack() as st:
        def sb(name, shape, dt=FP32):
            return tile(st, name, shape, dt)
        lst = sb("lst", [P, full + 1, P])
        cnt_i = sb("cnt_i", [P, E], I32)
        blk_i = sb("blk_i", [P, E], I32)
        blk = sb("blk", [P, E])
        blk_d = sb("blk_d", [P, E])
        blk_col = sb("blk_col", [P, 1])
        end_col = sb("end_col", [P, 1])
        iota_b = sb("iota_b", [P, NBLK])
        ge = sb("ge", [P, NBLK])
        e_row = sb("e_row", [1, NBLK])
        c_row = sb("c_row", [1, NBLK])
        s_lst = [sem("s_lst0"), sem("s_lst1")]
        s_ib = sem("s_ib")
        s_blk = sem("s_blk")
        s_cum = sem("s_cum")
        s_own = sem("s_own")
        s_lt = sem("s_lt")
        s_li = sem("s_li")
        with nc.Block() as block:
            @block.sync
            def _(sp):
                sp.dma_start(lst[:, 0:full, :], rows[0:full * P, :].rearrange("(n p) t -> p n t", p=P)).then_inc(s_lst[0], 16)
                sp.dma_start(lst[0:rest, full, :], rows[full * P:LCOLS, :]).then_inc(s_lst[1], 16)
                sp.wait_ge(s_lst[0], 16)
                sp.wait_ge(s_lst[1], 16)

            @block.gpsimd
            def _(pool):
                nc.gpsimd.iota(iota_b[:], [[1, NBLK]], base=0, channel_multiplier=0,
                               allow_small_or_imprecise_dtypes=True).then_inc(s_ib, 1)

            @block.vector
            def _(dve):
                own = Order(dve, s_own, 0)
                own.begin(0)
                tt, ts = nc.vector.tensor_tensor, nc.vector.tensor_scalar
                own.mark(ts(cnt_i[:], count[:], float(P - 1), None, ALU.add))
                own.wait()
                own.mark(nc.vector.tensor_single_scalar(blk_i[:], cnt_i[:], 7, ALU.arith_shift_right))
                own.wait()
                own.mark(ts(blk[:], blk_i[:], 1.0, None, ALU.max))
                own.wait()
                own.mark(tt(blk_d[0:E, :], blk[0:E, :], ident[0:E, 0:E], ALU.mult))
                own.wait()
                nc.vector.tensor_reduce(blk_col[0:E, :], blk_d[0:E, :], AX.X, ALU.add).then_inc(s_blk, 1)
                dve.wait_ge(s_cum, 1)
                own.mark(nc.vector.tensor_copy(end_col[0:E, :], half(0)[0:E, 0:1]))
                own.wait()
                dve.wait_ge(s_ib, 1)
                ts(ge[0:E - 1, :], iota_b[0:E - 1, :], end_col[0:E - 1, :], None, ALU.is_ge).then_inc(s_blk, 1)
                nc.vector.tensor_copy(tab_end[:], half(1)[0:1, 0:E])
                ts(base[:], half(2)[:, 0:E], float(P), None, ALU.mult)
                dve.wait_ge(s_cum, 2)
                for j in range(2):
                    s = slice(j * NB2, (j + 1) * NB2)
                    nc.vector.tensor_copy(tab_e[:, s], half(4 + j)[0:1, 0:NB2])
                    own.mark(nc.vector.tensor_copy(e_row[:, s], half(4 + j)[0:1, 0:NB2]))
                    own.mark(tt(c_row[:, s], iota_b[0:1, s], half(6 + j)[0:1, 0:NB2], ALU.subtract))
                    own.wait()
                    nc.vector.scalar_tensor_tensor(out=tab_col[:, s], in0=e_row[:, s], scalar=float(SEG // P),
                                                   in1=c_row[:, s], op0=ALU.mult, op1=ALU.add).then_inc(s_blk, 1)
                for g in range(full // 4 + 1):
                    dve.wait_ge(s_lt, g + 1)
                    n = 4 * P if g < full // 4 else rest
                    nc.vector.tensor_copy(idx[:, g * 4 * P:g * 4 * P + n], half(g % 4)[:, 0:n]).then_inc(s_li, 1)

            @block.tensor
            def _(pe):
                pe.wait_ge(s_blk, 1)
                bc = blk_col[0:E, 0:1].to_broadcast([E, P])
                nc.tensor.matmul(half(0)[0:E, 0:1], tri[0:E, 0:E], blk_col[0:E, :], start=True, stop=True)
                nc.tensor.matmul(half(1)[:, 0:E], bc, tri[0:E, 0:E], start=True, stop=True)
                nc.tensor.matmul(half(2)[:, 0:E], bc, tri_strict[0:E, 0:E], start=True, stop=True).then_inc(s_cum, 1)
                pe.wait_ge(s_blk, 2)
                for j in range(2):
                    rhs = ge[0:E - 1, j * NB2:(j + 1) * NB2]
                    nc.tensor.matmul(half(4 + j)[:, 0:NB2], ones[0:E - 1, :], rhs, start=True, stop=True)
                    last = nc.tensor.matmul(half(6 + j)[:, 0:NB2], blk_col[0:E - 1, 0:1].to_broadcast([E - 1, P]),
                                            rhs, start=True, stop=True)
                last.then_inc(s_cum, 1)
                pe.wait_ge(s_blk, 4)
                pe.wait_ge(s_lst[0], 16)
                pe.wait_ge(s_lst[1], 16)
                for g in range(full // 4 + 1):
                    at_least(pe, s_li, g - 3)
                    if g < full // 4:
                        for i in range(4):
                            last = nc.tensor.transpose(half(g % 4)[:, i * P:(i + 1) * P], lst[:, 4 * g + i, :], ident[:])
                    else:
                        last = nc.tensor.transpose(half(g % 4)[:, 0:rest], lst[0:rest, full, :], ident[0:rest, 0:rest])
                    last.then_inc(s_lt, 1)
    return dict(idx=idx, tab_e=tab_e, tab_col=tab_col, tab_end=tab_end, base=base, rows=out_rows)


def experts(nc, top, sem, tile, bank, half, env, tab):
    ident, h2_dram, y_dram, w_d = env["ident"], env["h2_dram"], env["y_dram"], env["w_experts"]
    SLOTS, WSLOTS = 4, 3
    passed = env["sems"]["passed"]
    idx, tab_e, tab_col, tab_end = tab["idx"], tab["tab_e"], tab["tab_col"], tab["tab_end"]
    iota_e, base, out_rows = env["iota_e"], tab["base"], tab["rows"]
    top_e, top_r = (env[k][:].rearrange("p n k -> p (n k)") for k in ("top_e", "top_r"))
    with ExitStack() as st:
        def sb(name, shape, dt=FP32):
            return tile(st, name, shape, dt)
        w = sb("w_exp", [P, WSLOTS, WPE])
        w_flat = w[:].rearrange("p s n -> p (s n)")
        place = sb("place", [P, SLOTS], I32)
        xg = sb("xg_e", [P, SLOTS, DM])
        x_t = sb("x_t", [P, 2, KD * P])
        th = sb("th_e", [P, 2, FF])
        hs = sb("hs_e", [P, 2, FF])
        h = sb("h_e", [P, 2, FF])
        h_t = sb("h_t", [P, 2, KF * P])
        y = sb("y_e", [P, SLOTS, DM])
        w_in = [sem(f"w_in{i}") for i in range(WSLOTS)]
        g_in = [sem(f"g_in{i}") for i in range(SLOTS)]
        y_st = [sem(f"y_st{i}") for i in range(SLOTS)]
        pick = sb("pick_e", [P, EXPERTS])
        first = sb("first_e", [P, 1])
        names = "w_ready place_done xT_ps xT_sb gu_ps gu_th silu h_done hT_ps hT_sb y_ps y_sb row_own".split()
        S = {n: sem("e_" + n) for n in names}

        def entry(t, i):
            return t[0:1, i:i + 1] if isinstance(i, int) else t[0:1, bass.ds(i, 1)]

        def steps(eng, step):
            for b in range(-1, SLOTS):
                step(b, b % SLOTS)
            with eng.Fori(SLOTS, NBLK - 2 * SLOTS + 1, SLOTS) as b:
                for q in range(SLOTS):
                    step(b + q, q)
            for b in range(NBLK - SLOTS, NBLK + 2):
                step(b, b % SLOTS)

        def valid(b):
            return not isinstance(b, int) or 0 <= b < NBLK

        with nc.Block() as block:
            @block.sync
            def _(sp):
                def load(e, k):
                    if not (isinstance(e, int) and e < WSLOTS):
                        sp.wait_ge(S["y_ps"], sp.value_load(entry(tab_end, e - WSLOTS), min_val=1, max_val=NBLK))
                    src = w_d[e, :, :] if isinstance(e, int) else w_d[bass.ds(e, 1), :, :].rearrange("a p n -> (a p) n")
                    sp.dma_start(w[:, k, :], src).then_inc(w_in[k], 16)

                def publish(e, k):
                    sp.wait_ge(w_in[k], 16 * (e // WSLOTS + 1))
                    sp.sem_inc(S["w_ready"], 1)

                load(0, 0)
                for e in range(WSLOTS - 1):
                    load(e + 1, e + 1)
                    publish(e, e)
                with sp.Fori(WSLOTS, EXPERTS - WSLOTS, WSLOTS) as e:
                    for k in range(WSLOTS):
                        load(e + k, k)
                        publish(e + k - 1, (k - 1) % WSLOTS)
                load(EXPERTS - 1, (EXPERTS - 1) % WSLOTS)
                publish(EXPERTS - 2, (EXPERTS - 2) % WSLOTS)
                publish(EXPERTS - 1, (EXPERTS - 1) % WSLOTS)

            @block.gpsimd
            def _(pool):
                def fetch(b, q):
                    column = pool.value_load(entry(tab_col, b), min_val=0, max_val=LCOLS - 1)
                    at_least(pool, g_in[q], 16 * (b // SLOTS))
                    nc.gpsimd.tensor_copy(place[:, q:q + 1], idx[:, bass.ds(column, 1)]).then_inc(S["place_done"], 1)
                    pool.wait_ge(S["place_done"], b + 1)
                    at_least(pool, S["xT_ps"], b - SLOTS + 1)
                    pool.sem_inc(passed, 1)
                    pool.indirect_dma_start(xg[:, q, :], None, h2_dram,
                                            bass.IndirectOffsetOnAxis(ap=place[:, q:q + 1], axis=0)).then_inc(g_in[q], 16)

                for b in range(SLOTS):
                    fetch(b, b)
                with pool.Fori(SLOTS, NBLK - SLOTS + 1, SLOTS) as b:
                    for q in range(SLOTS):
                        fetch(b + q, q)

            @block.tensor
            def _(pe):
                def weights(b):
                    e = pe.value_load(entry(tab_e, b), min_val=0, max_val=EXPERTS - 1)
                    return e, e % WSLOTS

                def step(b, q):
                    nxt, prev = b + 1, b - 1
                    if valid(nxt):
                        r = (q + 1) % SLOTS
                        pe.wait_ge(g_in[r], 16 * (nxt // SLOTS + 1))
                        at_least(pe, S["xT_sb"], nxt - 1)
                        for k in range(KD):
                            last = nc.tensor.transpose(half(r % 2)[:, k * P:(k + 1) * P], xg[:, r, k * P:(k + 1) * P], ident[:])
                        last.then_inc(S["xT_ps"], 1)
                    if valid(prev):
                        r = (q + 1) % 2
                        pe.wait_ge(S["h_done"], prev + 1)
                        at_least(pe, S["hT_sb"], prev - 1)
                        for k in range(KF):
                            last = nc.tensor.transpose(half(4 + r)[:, k * P:(k + 1) * P], h[:, r, k * P:(k + 1) * P], ident[:])
                        last.then_inc(S["hT_ps"], 1)
                    if valid(b):
                        r = q % 2
                        e, slot = weights(b)
                        pe.wait_ge(S["w_ready"], e + 1)
                        pe.wait_ge(S["xT_sb"], b + 1)
                        at_least(pe, S["h_done"], b - 1)
                        for k in range(KD):
                            last = nc.tensor.matmul(half(2 + r), x_t[:, r, k * P:(k + 1) * P],
                                                    w_flat[:, bass.ds(slot * WPE + k * 2 * FF, 2 * FF)],
                                                    start=(k == 0), stop=(k == KD - 1))
                        last.then_inc(S["gu_ps"], 1)
                    if valid(prev):
                        r = (q + 1) % 2
                        e, slot = weights(prev)
                        pe.wait_ge(S["hT_sb"], prev + 1)
                        at_least(pe, S["y_sb"], prev - 1)
                        for k in range(KF):
                            last = nc.tensor.matmul(half(6 + r), h_t[:, r, k * P:(k + 1) * P],
                                                    w_flat[:, bass.ds(slot * WPE + KD * 2 * FF + k * DM, DM)],
                                                    start=(k == 0), stop=(k == KF - 1))
                        last.then_inc(S["y_ps"], 1)

                steps(pe, step)

            @block.scalar
            def _(act):
                def step(b, q):
                    nxt, prev, old = b + 1, b - 1, b - 2
                    if valid(nxt):
                        r = (q + 1) % 2
                        act.wait_ge(S["xT_ps"], nxt + 1)
                        at_least(act, S["gu_ps"], nxt - 1)
                        nc.scalar.copy(x_t[:, r, :], half(r)).then_inc(S["xT_sb"], 1)
                    if valid(b):
                        r = q % 2
                        act.wait_ge(S["gu_ps"], b + 1)
                        at_least(act, S["silu"], b - 1)
                        nc.scalar.activation(th[:, r, :], half(2 + r)[:, 0:FF], ACT.Tanh, scale=0.5).then_inc(S["gu_th"], 1)
                    if valid(prev):
                        r = (q - 1) % SLOTS
                        act.wait_ge(S["y_ps"], prev + 1)
                        at_least(act, y_st[r], 16 * (prev // SLOTS))
                        nc.scalar.copy(y[:, r, :], half(6 + r % 2)).then_inc(S["y_sb"], 1)
                    if valid(old):
                        r = (q - 2) % SLOTS
                        act.wait_ge(S["y_sb"], old + 1)
                        dst = y_dram[old * P:(old + 1) * P, :] if isinstance(old, int) else y_dram[bass.ds(old * P, P), :]
                        act.dma_start(dst, y[:, r, :]).then_inc(y_st[r], 16)

                steps(act, step)
                for q in range(SLOTS):
                    act.wait_ge(y_st[q], 16 * NBLK // SLOTS)

            @block.vector
            def _(dve):
                found = Order(dve, S["row_own"], 2)

                def step(b, q):
                    prev = b - 1
                    if valid(prev):
                        r = (q + 1) % 2
                        dve.wait_ge(S["hT_ps"], prev + 1)
                        at_least(dve, S["y_ps"], prev - 1)
                        nc.vector.tensor_copy(h_t[:, r, :], half(4 + r)[:, 0:KF * P]).then_inc(S["hT_sb"], 1)
                    if valid(b):
                        r = q % 2
                        dve.wait_ge(S["gu_th"], b + 1)
                        nc.vector.scalar_tensor_tensor(out=hs[:, r, :], in0=th[:, r, :], scalar=1.0, in1=half(2 + r)[:, 0:FF],
                                                       op0=ALU.add, op1=ALU.mult).then_inc(S["silu"], 1)
                        dve.wait_ge(S["silu"], b + 1)
                        at_least(dve, S["hT_ps"], b - 1)
                        nc.vector.tensor_tensor(h[:, r, :], hs[:, r, :], half(2 + r)[:, FF:2 * FF], ALU.mult).then_inc(S["h_done"], 1)
                        i = b * (NCH * TOPK) // NBLK
                        at = slice(i, i + 1) if isinstance(b, int) else bass.ds(i, 1)
                        found.begin(b)
                        found.mark(nc.vector.scalar_tensor_tensor(out=pick[:], in0=iota_e[:], scalar=top_e[:, at], in1=base[:],
                                                                  op0=ALU.is_equal, op1=ALU.mult))
                        found.wait()
                        found.mark(nc.vector.tensor_reduce(first[:], pick[:], AX.X, ALU.add))
                        found.wait()
                        found.end()
                        nc.vector.tensor_tensor(out_rows[:, at], first[:], top_r[:, at], ALU.add)

                steps(dve, step)


def combine(nc, top, sem, tile, bank, half, env, tab):
    ident, mod_dram, top_w, rows = env["ident"], env["mod_dram"], env["top_w"], tab["rows"]
    x1_dram, h2_dram, y_dram, out = env["x1_dram"], env["h2_dram"], env["y_dram"], env["out"]
    passed = env["sems"]["passed"]
    SLOTS = 4
    with ExitStack() as st:
        def sb(name, shape, dt=FP32):
            return tile(st, name, shape, dt)
        w = sb("w_sh", [P, WPE])
        gate = sb("gate_c", [P, BATCH, DM])
        h2 = sb("h2_c", [P, 2, DM])
        x1 = sb("x1_c", [P, 2, DM])
        x_t = sb("x_tc", [P, 2, KD * P])
        th = sb("th_c", [P, 2, FF])
        hs = sb("hs_c", [P, 2, FF])
        h = sb("h_c", [P, 2, FF])
        h_t = sb("h_tc", [P, 2, KF * P])
        place = sb("place_c", [P, SLOTS, TOPK], I32)
        g = sb("g_c", [P, SLOTS, TOPK, DM])
        acc = sb("acc_c", [P, SLOTS, DM])
        acc2 = sb("acc2_c", [P, 2, DM])
        gated = sb("gated_c", [P, 2, DM])
        o = sb("o_c", [P, 2, DM])
        w_in = sem("c_w_in")
        h2_in = [sem(f"c_h2_in{i}") for i in range(2)]
        x1_in = [sem(f"c_x1_in{i}") for i in range(2)]
        g_in = [sem(f"c_g_in{i}") for i in range(SLOTS)]
        o_st = [sem(f"c_o_st{i}") for i in range(2)]
        names = "place_done xT_ps xT_sb gu_ps gu_th silu h_done hT_ps hT_sb y_ps y_sb second o_done dve_s".split()
        S = {n: sem("c_" + n) for n in names}

        def rows_of(dram, chunk):
            return dram[chunk * P:(chunk + 1) * P, :] if isinstance(chunk, int) else dram[bass.ds(chunk * P, P), :]

        def columns(t, chunk, first, n):
            i = chunk * TOPK + first
            return t[:, i:i + n] if isinstance(chunk, int) else t[:, bass.ds(i, n)]

        weights = top_w[:].rearrange("p n k -> p (n k)")

        def steps(eng, step):
            for t in range(-1, SLOTS):
                step(t, t % SLOTS)
            with eng.Fori(SLOTS, NCH - 2 * SLOTS + 1, SLOTS) as t:
                for q in range(SLOTS):
                    step(t + q, q)
            for t in range(NCH - SLOTS, NCH + 3):
                step(t, t % SLOTS)

        def valid(t):
            return not isinstance(t, int) or 0 <= t < NCH

        with nc.Block() as block:
            @block.sync
            def _(sp):
                def step(t, q):
                    nxt, prev, old = t + 1, t - 1, t - 3
                    if valid(nxt):
                        r = (q + 1) % 2
                        at_least(sp, S["xT_ps"], nxt - 1)
                        sp.dma_start(h2[:, r, :], rows_of(h2_dram, nxt)).then_inc(h2_in[r], 16)
                    if isinstance(t, int) and t == -1:
                        sp.dma_start(w[:], env["w_shared"]).then_inc(w_in, 16)
                        for b in range(BATCH):
                            sp.dma_start(gate[:, b, :], mod_dram[b:b + 1, 5 * DM:6 * DM].broadcast_to([P, DM])).then_inc(w_in, 16)
                    if valid(prev):
                        r = (q - 1) % 2
                        at_least(sp, S["o_done"], prev - 1)
                        sp.dma_start(x1[:, r, :], rows_of(x1_dram, prev)).then_inc(x1_in[r], 16)
                    if valid(old):
                        r = (q - 3) % 2
                        sp.wait_ge(S["o_done"], old + 1)
                        sp.dma_start(rows_of(out, old), o[:, r, :]).then_inc(o_st[r], 16)

                steps(sp, step)
                for q in range(2):
                    sp.wait_ge(o_st[q], 16 * NCH // 2)

            @block.gpsimd
            def _(pool):
                def fetch(t, q):
                    at_least(pool, g_in[q], 16 * TOPK * (t // SLOTS))
                    nc.gpsimd.tensor_copy(place[:, q, :], columns(rows, t, 0, TOPK)).then_inc(S["place_done"], 1)
                    pool.wait_ge(S["place_done"], t + 1)
                    at_least(pool, S["o_done"], t - SLOTS + 1)
                    pool.sem_inc(passed, 1)
                    for k in range(TOPK):
                        pool.indirect_dma_start(g[:, q, k, :], None, y_dram,
                                                bass.IndirectOffsetOnAxis(ap=place[:, q, k:k + 1], axis=0)).then_inc(g_in[q], 16)

                for t in range(SLOTS):
                    fetch(t, t)
                with pool.Fori(SLOTS, NCH - SLOTS + 1, SLOTS) as t:
                    for q in range(SLOTS):
                        fetch(t + q, q)

            @block.tensor
            def _(pe):
                def step(t, q):
                    nxt, prev = t + 1, t - 1
                    if valid(nxt):
                        r = (q + 1) % 2
                        pe.wait_ge(h2_in[r], 16 * (nxt // 2 + 1))
                        at_least(pe, S["xT_sb"], nxt - 1)
                        for k in range(KD):
                            last = nc.tensor.transpose(half(r)[:, k * P:(k + 1) * P], h2[:, r, k * P:(k + 1) * P], ident[:])
                        last.then_inc(S["xT_ps"], 1)
                    if valid(t):
                        r = q % 2
                        if isinstance(t, int) and t == 0:
                            pe.wait_ge(w_in, 16 * (1 + BATCH))
                        pe.wait_ge(S["xT_sb"], t + 1)
                        at_least(pe, S["h_done"], t - 1)
                        for k in range(KD):
                            last = nc.tensor.matmul(half(2 + r), x_t[:, r, k * P:(k + 1) * P], w[:, k * 2 * FF:(k + 1) * 2 * FF],
                                                    start=(k == 0), stop=(k == KD - 1))
                        last.then_inc(S["gu_ps"], 1)
                    if valid(prev):
                        r = (q + 1) % 2
                        pe.wait_ge(S["h_done"], prev + 1)
                        at_least(pe, S["hT_sb"], prev - 1)
                        for k in range(KF):
                            last = nc.tensor.transpose(half(4 + r)[:, k * P:(k + 1) * P], h[:, r, k * P:(k + 1) * P], ident[:])
                        last.then_inc(S["hT_ps"], 1)
                        pe.wait_ge(S["hT_sb"], prev + 1)
                        at_least(pe, S["y_sb"], prev - 1)
                        for k in range(KF):
                            last = nc.tensor.matmul(half(6 + r), h_t[:, r, k * P:(k + 1) * P],
                                                    w[:, KD * 2 * FF + k * DM:KD * 2 * FF + (k + 1) * DM],
                                                    start=(k == 0), stop=(k == KF - 1))
                        last.then_inc(S["y_ps"], 1)

                steps(pe, step)

            @block.scalar
            def _(act):
                def step(t, q):
                    nxt, prev, old = t + 1, t - 1, t - 2
                    if valid(nxt):
                        r = (q + 1) % 2
                        act.wait_ge(S["xT_ps"], nxt + 1)
                        at_least(act, S["gu_ps"], nxt - 1)
                        nc.scalar.copy(x_t[:, r, :], half(r)).then_inc(S["xT_sb"], 1)
                    if valid(t):
                        r = q % 2
                        act.wait_ge(S["gu_ps"], t + 1)
                        at_least(act, S["silu"], t - 1)
                        nc.scalar.activation(th[:, r, :], half(2 + r)[:, 0:FF], ACT.Tanh, scale=0.5).then_inc(S["gu_th"], 1)
                    if valid(prev):
                        r = (q + 1) % 2
                        act.wait_ge(S["hT_ps"], prev + 1)
                        at_least(act, S["y_ps"], prev - 1)
                        nc.scalar.copy(h_t[:, r, :], half(4 + r)[:, 0:KF * P]).then_inc(S["hT_sb"], 1)
                        act.wait_ge(S["y_ps"], prev + 1)
                        at_least(act, S["o_done"], prev - SLOTS + 1)
                        nc.scalar.mul(acc[:, (q - 1) % SLOTS, :], half(6 + r), 0.5).then_inc(S["y_sb"], 1)
                    if valid(old):
                        r = (q - 2) % SLOTS
                        act.wait_ge(g_in[r], 16 * TOPK * (old // SLOTS + 1))
                        at_least(act, S["o_done"], old - 1)
                        nc.scalar.mul(acc2[:, r % 2, :], g[:, r, 1, :], columns(weights, old, 1, 1)).then_inc(S["second"], 1)

                steps(act, step)

            @block.vector
            def _(dve):
                total = Order(dve, S["dve_s"], TOPK + 1)

                def step(t, q):
                    old = t - 2
                    if valid(t):
                        r = q % 2
                        dve.wait_ge(S["gu_th"], t + 1)
                        nc.vector.scalar_tensor_tensor(out=hs[:, r, :], in0=th[:, r, :], scalar=1.0, in1=half(2 + r)[:, 0:FF],
                                                       op0=ALU.add, op1=ALU.mult).then_inc(S["silu"], 1)
                        dve.wait_ge(S["silu"], t + 1)
                        at_least(dve, S["hT_ps"], t - 1)
                        nc.vector.tensor_tensor(h[:, r, :], hs[:, r, :], half(2 + r)[:, FF:2 * FF], ALU.mult).then_inc(S["h_done"], 1)
                    if valid(old):
                        r = (q - 2) % SLOTS
                        sums = (acc[:, r, :], acc2[:, r % 2, :])
                        b = old // CPB
                        gb = (gate[:, b, :] if isinstance(old, int) else
                              gate[:].rearrange("p b d -> p (b d)")[:, bass.ds(b * DM, DM)])
                        total.begin(old)
                        dve.wait_ge(g_in[r], 16 * TOPK * (old // SLOTS + 1))
                        dve.wait_ge(S["y_sb"], old + 1)
                        for i, k in enumerate((0, 2, 3, 4, 5, 6, 7)):
                            if i == 1:
                                dve.wait_ge(S["second"], old + 1)
                            if i >= 2:
                                total.wait(i - 1)
                            total.mark(nc.vector.scalar_tensor_tensor(out=sums[i % 2], in0=g[:, r, k, :], scalar=columns(weights, old, k, 1),
                                                                      in1=sums[i % 2], op0=ALU.mult, op1=ALU.add))
                        total.wait()
                        total.mark(nc.vector.tensor_tensor(acc[:, r, :], acc[:, r, :], acc2[:, r % 2, :], ALU.add))
                        total.wait()
                        if isinstance(old, int) and old == 0:
                            dve.wait_ge(w_in, 16 * (1 + BATCH))
                        total.mark(nc.vector.tensor_tensor(gated[:, r % 2, :], acc[:, r, :], gb, ALU.mult))
                        total.wait()
                        total.end()
                        dve.wait_ge(x1_in[r % 2], 16 * (old // 2 + 1))
                        at_least(dve, o_st[r % 2], 16 * (old // 2))
                        nc.vector.tensor_tensor(o[:, r % 2, :], gated[:, r % 2, :], x1[:, r % 2, :], ALU.add).then_inc(S["o_done"], 1)

                steps(dve, step)


def kernel(**inputs):
    import numpy as _np
    import concourse.bacc as _bacc
    from concourse import mybir as _mybir
    from concourse.bass_utils import run_bass_kernel_spmd as _run

    a = {k: _np.asarray(v) for k, v in inputs.items()}

    def parts(m):
        return m.reshape(m.shape[0] // P, P, m.shape[1]).transpose(1, 0, 2)

    def spread(v):
        return _np.broadcast_to(v, (P, v.shape[0]))

    def expert(gate, up, down):
        n = gate.shape[0]
        gu = _np.concatenate([gate, up], axis=2).reshape(n, KD, P, 2 * FF).transpose(0, 2, 1, 3).reshape(n, P, KD * 2 * FF)
        dn = down.reshape(n, KF, P, DM).transpose(0, 2, 1, 3).reshape(n, P, KF * DM)
        return _np.concatenate([gu, dn], axis=2)

    arrays = {
        "x": a["L0_attn_x"].reshape(TOKENS, DM),
        "c_t": parts(a["L0_c"].T),
        "w_mod": parts(a["L0_wmod"]),
        "w_in": parts(a["L0_attn_in_proj_w"].T),
        "conv_w": parts(a["L0_attn_conv_w"]),
        "conv_b": a["L0_attn_conv_b"].reshape(NE, P).T,
        "dt_bias": spread(a["L0_attn_dt_bias"]),
        "a_log": spread(a["L0_attn_A_log"]),
        "d_skip": spread(a["L0_attn_D"]),
        "norm_w": a["L0_attn_norm_w"].reshape(KD, P).T,
        "gnorm_w": a["L0_attn_gnorm_w"].reshape(KI, P).T,
        "w_out": parts(a["L0_attn_out_proj_w"].T),
        "w_router": parts(a["L0_ffn_w_router"]),
        "b_router": spread(a["L0_ffn_b_router"]),
        "w_experts": expert(a["L0_ffn_we_gate"], a["L0_ffn_we_up"], a["L0_ffn_we_down"]),
        "w_shared": expert(a["L0_ffn_ws_gate"][None], a["L0_ffn_ws_up"][None], a["L0_ffn_ws_down"][None])[0],
    }
    arrays = {f"in_{k}_dram": _np.ascontiguousarray(v) for k, v in arrays.items()}
    nc = _bacc.Bacc("TRN2", target_bir_lowering=False, num_devices=1)
    args = [nc.dram_tensor(k, v.shape, _mybir.dt.from_np(v.dtype), kind="ExternalInput").ap() for k, v in arrays.items()]
    args.append(nc.dram_tensor("out_0_dram", (TOKENS, DM), _mybir.dt.float32, kind="ExternalOutput").ap())
    program(nc, *args)
    r = _run(nc, [arrays], core_ids=[0])
    return r.results[0]["out_0_dram"].reshape(BATCH, SEQ, DM)
```
